# Optimizing a Trainium2 kernel written in Bass

```python
import numpy as np
import jax
import jax.numpy as jnp

def _softmax(x, axis=-1):
    return jax.nn.softmax(x, axis=axis)

def _gelu(x):
    return jax.nn.gelu(x, approximate=True)

def _silu(x):
    return jax.nn.silu(x)

def _sigmoid(x):
    return jax.nn.sigmoid(x)

def _layernorm(x, axis=-1, eps=1e-05):
    m = jnp.mean(x, axis=axis, keepdims=True)
    v = jnp.var(x, axis=axis, keepdims=True)
    return (x - m) / jnp.sqrt(v + eps)

def _scatter_add(tgt, idx, src, axis=0):
    return tgt.at[idx].add(src)

def _segment_sum(src, seg, n):
    return jax.ops.segment_sum(src, seg, n)
kernel_name = 'mk_gnn_ffn_d2_gnn_r8_67bfbb'

def setup_inputs(seed: int=0):
    np.random.seed(seed)
    _w = jnp.asarray

    def _rec_inputs():
        import jax
        import jax.numpy as jnp
        _gk = jax.random.key(seed)
        x = -6.415e-05 + 1 * jax.random.normal(jax.random.fold_in(_gk, 1), (1250, 1024), jnp.float32)
        src = jax.random.randint(jax.random.fold_in(_gk, 2), (40000,), 0, 1250, jnp.int32)
        dst = jnp.minimum((1250 * jax.random.uniform(jax.random.fold_in(_gk, 3), (40000,)) ** 2.0).astype(jnp.int32), 9999)
        _o = jnp.argsort(dst, stable=True)
        src = src[_o]
        dst = dst[_o]
        return (x, src, dst)
    x, src, dst = _rec_inputs()

    def _L0_gnn_setup():
        import jax, jax.numpy as jnp
        import numpy as np
        N_NODES = 1250
        N_EDGES = 20000
        DIM = 1024
        key = jax.random.key(seed)
        k1, k2, k3 = jax.random.split(key, 3)
        x = jax.random.normal(k1, (N_NODES, DIM), dtype=jnp.float32)
        edge_index = jax.random.randint(k2, (2, N_EDGES), 0, N_NODES, dtype=jnp.int64)
        W = jax.random.normal(k3, (DIM, DIM), dtype=jnp.float32) * (1.0 / np.sqrt(DIM))
        b = jnp.zeros((DIM,), dtype=jnp.float32)
        return {'x': x, 'edge_index': edge_index, 'W': W, 'b': b}
    _L0_gnn_all = _L0_gnn_setup()
    _L0_gnn_in = {k: v for k, v in _L0_gnn_all.items() if k in ('W', 'b')}
    del _L0_gnn_all

    def _L0_ffn_setup():
        import jax, jax.numpy as jnp
        import numpy as np
        SEQ, BATCH, D_IN, D_LAT = (512, 64, 1024, 1024)
        key = jax.random.key(seed)
        ks = jax.random.split(key, 5)
        scale = 0.02
        d_cat = D_IN + D_LAT
        return {'x': jax.random.normal(ks[0], (SEQ, BATCH, D_IN), dtype=jnp.float32), 'W_f': jax.random.normal(ks[1], (D_LAT, d_cat), dtype=jnp.float32) * scale, 'b_f': jnp.zeros((D_LAT,), dtype=jnp.float32), 'W_i': jax.random.normal(ks[2], (D_LAT, d_cat), dtype=jnp.float32) * scale, 'b_i': jnp.zeros((D_LAT,), dtype=jnp.float32), 'W_o': jax.random.normal(ks[3], (D_LAT, d_cat), dtype=jnp.float32) * scale, 'b_o': jnp.zeros((D_LAT,), dtype=jnp.float32), 'W_c': jax.random.normal(ks[4], (D_LAT, d_cat), dtype=jnp.float32) * scale, 'b_c': jnp.zeros((D_LAT,), dtype=jnp.float32)}
    _L0_ffn_all = _L0_ffn_setup()
    _L0_ffn_in = {k: v for k, v in _L0_ffn_all.items() if k in ('W_f', 'b_f', 'W_i', 'b_i', 'W_o', 'b_o', 'W_c', 'b_c')}
    del _L0_ffn_all

    def _L1_gnn_setup():
        import jax, jax.numpy as jnp
        import numpy as np
        N_NODES = 3125
        N_EDGES = 50000
        D = 1024

        def _sage_layer(h, edge_src, edge_dst, deg_inv, W_self, W_neigh, b):
            msg = h[edge_src]
            agg = jax.ops.segment_sum(msg, edge_dst, num_segments=h.shape[0])
            mean = agg * deg_inv[:, None]
            return h @ W_self + mean @ W_neigh + b
        key = jax.random.key(seed)
        ks = jax.random.split(key, 8)
        s = 1.0 / np.sqrt(D)
        return {'x': jax.random.normal(ks[0], (N_NODES, D), dtype=jnp.float32), 'edge_src': jax.random.randint(ks[1], (N_EDGES,), 0, N_NODES, dtype=jnp.int32), 'edge_dst': jax.random.randint(ks[2], (N_EDGES,), 0, N_NODES, dtype=jnp.int32), 'W_self0': jax.random.normal(ks[3], (D, D), dtype=jnp.float32) * s, 'W_neigh0': jax.random.normal(ks[4], (D, D), dtype=jnp.float32) * s, 'b0': jnp.zeros((D,), dtype=jnp.float32), 'W_self1': jax.random.normal(ks[5], (D, D), dtype=jnp.float32) * s, 'W_neigh1': jax.random.normal(ks[6], (D, D), dtype=jnp.float32) * s, 'b1': jnp.zeros((D,), dtype=jnp.float32)}
    _L1_gnn_all = _L1_gnn_setup()
    _L1_gnn_in = {k: v for k, v in _L1_gnn_all.items() if k in ('W_self0', 'W_neigh0', 'b0', 'W_self1', 'W_neigh1', 'b1')}
    del _L1_gnn_all

    def _L1_ffn_setup():
        import jax, jax.numpy as jnp
        import numpy as np
        THRESHOLD = 0.1
        key = jax.random.key(seed)
        k1, k2, k3 = jax.random.split(key, 3)
        B, S, D, E = (4, 512, 1024, 8)
        inputs = jax.random.normal(k1, (B, S, D), dtype=jnp.float32)
        gate_w = jax.random.normal(k2, (D, E), dtype=jnp.float32) * 0.02
        gate_b = jnp.zeros((E,), dtype=jnp.float32)
        expert_w = jax.random.normal(k3, (E, D, D), dtype=jnp.float32) * 0.02
        expert_b = jnp.zeros((E, D), dtype=jnp.float32)
        return {'inputs': inputs, 'gate_w': gate_w, 'gate_b': gate_b, 'expert_w': expert_w, 'expert_b': expert_b}
    _L1_ffn_all = _L1_ffn_setup()
    _L1_ffn_in = {k: v for k, v in _L1_ffn_all.items() if k in ('gate_w', 'gate_b', 'expert_w', 'expert_b')}
    del _L1_ffn_all
    return {'x': x, 'src': src, 'dst': dst, 'L0_gnn_W': _L0_gnn_in['W'], 'L0_gnn_b': _L0_gnn_in['b'], 'L0_ffn_W_f': _L0_ffn_in['W_f'], 'L0_ffn_b_f': _L0_ffn_in['b_f'], 'L0_ffn_W_i': _L0_ffn_in['W_i'], 'L0_ffn_b_i': _L0_ffn_in['b_i'], 'L0_ffn_W_o': _L0_ffn_in['W_o'], 'L0_ffn_b_o': _L0_ffn_in['b_o'], 'L0_ffn_W_c': _L0_ffn_in['W_c'], 'L0_ffn_b_c': _L0_ffn_in['b_c'], 'L1_gnn_W_self0': _L1_gnn_in['W_self0'], 'L1_gnn_W_neigh0': _L1_gnn_in['W_neigh0'], 'L1_gnn_b0': _L1_gnn_in['b0'], 'L1_gnn_W_self1': _L1_gnn_in['W_self1'], 'L1_gnn_W_neigh1': _L1_gnn_in['W_neigh1'], 'L1_gnn_b1': _L1_gnn_in['b1'], 'L1_ffn_gate_w': _L1_ffn_in['gate_w'], 'L1_ffn_gate_b': _L1_ffn_in['gate_b'], 'L1_ffn_expert_w': _L1_ffn_in['expert_w'], 'L1_ffn_expert_b': _L1_ffn_in['expert_b']}

def reference(x, src, dst, L0_gnn_W, L0_gnn_b, L0_ffn_W_f, L0_ffn_b_f, L0_ffn_W_i, L0_ffn_b_i, L0_ffn_W_o, L0_ffn_b_o, L0_ffn_W_c, L0_ffn_b_c, L1_gnn_W_self0, L1_gnn_W_neigh0, L1_gnn_b0, L1_gnn_W_self1, L1_gnn_W_neigh1, L1_gnn_b1, L1_ffn_gate_w, L1_ffn_gate_b, L1_ffn_expert_w, L1_ffn_expert_b):
    import jax
    import jax.numpy as jnp

    def _L0_gnn_ref(x, edge_index, W, b):
        import jax, jax.numpy as jnp
        import numpy as np
        N_NODES = 1250
        N_EDGES = 20000
        DIM = 1024
        'GCNConv (add_self_loops=True, symmetric norm) -> Dropout(eval=identity) -> ReLU.'
        n = x.shape[0]
        loops = jnp.arange(n, dtype=edge_index.dtype)
        src = jnp.concatenate([edge_index[0], loops])
        dst = jnp.concatenate([edge_index[1], loops])
        deg = jax.ops.segment_sum(jnp.ones_like(dst, dtype=x.dtype), dst, num_segments=n)
        dinv = jnp.where(deg > 0, jax.lax.rsqrt(deg), jnp.zeros_like(deg))
        norm = dinv[src] * dinv[dst]
        h = x @ W
        msg = h[src] * norm[:, None]
        out = jax.ops.segment_sum(msg, dst, num_segments=n) + b
        return jax.nn.relu(out)

    def _L0_ffn_ref(x, W_f, b_f, W_i, b_i, W_o, b_o, W_c, b_c):
        import jax, jax.numpy as jnp
        import numpy as np
        SEQ, BATCH, D_IN, D_LAT = (512, 64, 1024, 1024)
        d_lat = W_f.shape[0]
        W_all = jnp.concatenate([W_f, W_i, W_o, W_c], axis=0)
        b_all = jnp.concatenate([b_f, b_i, b_o, b_c], axis=0)
        batch = x.shape[1]
        h0 = jnp.zeros((batch, d_lat), dtype=x.dtype)
        c0 = jnp.zeros((batch, d_lat), dtype=x.dtype)

        def step(carry, x_t):
            h, c = carry
            z = jnp.concatenate([h, x_t], axis=-1)
            gates = z @ W_all.T + b_all
            f_t = jax.nn.sigmoid(gates[:, 0 * d_lat:1 * d_lat])
            i_t = jax.nn.sigmoid(gates[:, 1 * d_lat:2 * d_lat])
            o_t = jax.nn.sigmoid(gates[:, 2 * d_lat:3 * d_lat])
            g_t = jnp.tanh(gates[:, 3 * d_lat:4 * d_lat])
            c_t = f_t * c + i_t * g_t
            h_t = o_t * jnp.tanh(c_t)
            return ((h_t, c_t), h_t)
        _, hidden_states = jax.lax.scan(step, (h0, c0), x)
        return hidden_states

    def _L1_gnn_ref(x, edge_src, edge_dst, W_self0, W_neigh0, b0, W_self1, W_neigh1, b1):
        import jax, jax.numpy as jnp
        import numpy as np
        N_NODES = 3125
        N_EDGES = 50000
        D = 1024

        def _sage_layer(h, edge_src, edge_dst, deg_inv, W_self, W_neigh, b):
            msg = h[edge_src]
            agg = jax.ops.segment_sum(msg, edge_dst, num_segments=h.shape[0])
            mean = agg * deg_inv[:, None]
            return h @ W_self + mean @ W_neigh + b
        N = x.shape[0]
        deg = jax.ops.segment_sum(jnp.ones_like(edge_dst, dtype=x.dtype), edge_dst, num_segments=N)
        deg_inv = 1.0 / jnp.maximum(deg, 1.0)
        h = jax.nn.relu(_sage_layer(x, edge_src, edge_dst, deg_inv, W_self0, W_neigh0, b0))
        out = _sage_layer(h, edge_src, edge_dst, deg_inv, W_self1, W_neigh1, b1)
        return out

    def _L1_ffn_ref(inputs, gate_w, gate_b, expert_w, expert_b):
        import jax, jax.numpy as jnp
        import numpy as np
        THRESHOLD = 0.1
        d = inputs.shape[-1]
        x = inputs.reshape(-1, d)
        gate_logits = jax.nn.softmax(x @ gate_w + gate_b, axis=-1)
        selected = (gate_logits >= THRESHOLD).astype(x.dtype)
        weights = gate_logits * selected
        wsum = jnp.sum(weights, axis=-1, keepdims=True)
        weights = weights / jnp.where(wsum == 0, jnp.ones_like(wsum), wsum)
        E = expert_w.shape[0]
        out = jnp.zeros((x.shape[0], expert_w.shape[-1]), dtype=x.dtype)
        for e in range(E):
            out = out + weights[:, e:e + 1] * (x @ expert_w[e] + expert_b[e])
        return out.reshape(*inputs.shape[:-1], out.shape[-1])
    edge_index = jnp.stack([src, dst])
    x = x + _L0_gnn_ref(_layernorm(x, axis=-1), edge_index, L0_gnn_W, L0_gnn_b)
    x = x + _L0_ffn_ref(_layernorm(x, axis=-1)[None], L0_ffn_W_f, L0_ffn_b_f, L0_ffn_W_i, L0_ffn_b_i, L0_ffn_W_o, L0_ffn_b_o, L0_ffn_W_c, L0_ffn_b_c)[0]
    x = x + _L1_gnn_ref(_layernorm(x, axis=-1), src, dst, L1_gnn_W_self0, L1_gnn_W_neigh0, L1_gnn_b0, L1_gnn_W_self1, L1_gnn_W_neigh1, L1_gnn_b1)
    x = x + _L1_ffn_ref(_layernorm(x, axis=-1)[None], L1_ffn_gate_w, L1_ffn_gate_b, L1_ffn_expert_w, L1_ffn_expert_b)[0]
    return x

_drawn_inputs = setup_inputs


def setup_inputs(seed=0):
    import zlib

    import numpy as np

    out = dict(_drawn_inputs(seed))
    spreads = {'L0_gnn_b': (0.0, 0.1),
     'L0_ffn_b_f': (0.0, 0.1),
     'L0_ffn_b_i': (0.0, 0.8),
     'L0_ffn_b_o': (0.0, 0.74),
     'L0_ffn_b_c': (0.0, 0.1),
     'L1_gnn_b0': (0.0, 0.1),
     'L1_gnn_b1': (0.0, 0.1),
     'L1_ffn_gate_b': (0.0, 0.1),
     'L1_ffn_expert_b': (0.0, 0.1)}
    factors = {}
    for name, (base, spread) in spreads.items():
        noise = np.random.default_rng([zlib.crc32(name.encode()), seed]).standard_normal(out[name].shape)
        drawn = base * np.exp(spread * noise) if base else spread * noise
        out[name] = jnp.asarray(drawn.astype(out[name].dtype))
    for name, factor in factors.items():
        out[name] = (out[name] * factor).astype(out[name].dtype)
    return out
```

```python
from contextlib import ExitStack

import concourse.bass as bass
from concourse import mybir

F32 = mybir.dt.float32
F32R = mybir.dt.float32r
BF16 = mybir.dt.bfloat16
U16 = mybir.dt.uint16
I32 = mybir.dt.int32
ALU = mybir.AluOpType
ACT = mybir.ActivationFunctionType
AX = mybir.AxisListType

NODES, DIM, EDGES, EXPERTS = 1250, 1024, 40000, 8
P = 125
TILES = NODES // P
KC = DIM // 128
HALF = DIM // 2
HALVES = 2
CHUNKS = EDGES // P
GROUPS = CHUNKS // 2
WIN = 25
WCOLS = WIN * TILES
MAX_ROUNDS = NODES // WIN
UNROLL = 4
LN_EPS = 1e-5
SAGE_LAYERS = 2
THRESHOLD = 0.1
EXACT = 4096

RING = 5
J_PREP = [0, 60, 140, 220, 300]
J_GCN, J_LSTM, J_SAGE, J_EXPERT_B, J_EXPERT = 20, 80, [160, 240], 320, 340
J_END = J_EXPERT + EXPERTS * 2 * TILES
N_GCN, N_LSTM, N_SAGE, N_MOE = 0, 2, [8, 12], 16


def build(nc, x, src_c, dst_c, dst_g, gcn_w, gcn_b, lstm_w, lstm_b, sage_wn, sage_ws, sage_b,
          gate_w, gate_b, expert_w, expert_b, out):
    ctx = ExitStack()
    with ctx:
        def dram(name, shape):
            return nc.dram_tensor(name, shape, F32, kind="Internal").ap()

        x1_d, x2_d, h1_d, x3_d = (dram(n, [NODES, DIM]) for n in ("x1_d", "x2_d", "h1_d", "x3_d"))
        ahi_d, alo_d = (dram(n, [TILES, P, TILES * P]) for n in ("ahi_d", "alo_d"))
        stat_d = dram("stat_d", [2, GROUPS])

        def rows(ap):
            return ap.rearrange("(t p) d -> t p d", p=P)

        x_t, x1_t, x2_t, h1_t, x3_t, out_t = map(rows, (x, x1_d, x2_d, h1_d, x3_d, out))

        def sem(name):
            return ctx.enter_context(nc.semaphore(name))

        base = 16512
        used = {}

        def at(name, shape, dt, offset):
            t = nc.alloc_sbuf_tensor_at(name, shape, dt, offset=offset)
            n = 1
            for s in shape[1:]:
                n *= s
            used[name] = offset + n * mybir.dt.size(dt)
            return t

        XT0 = base
        W0 = XT0 + 80000
        Z0 = W0 + 65536
        S0 = Z0 + 40960
        C0 = S0 + 22816
        xt_hi = at("xt_hi", [128, TILES, KC, P], F32R, XT0)
        xt_lo = at("xt_lo", [128, TILES, KC, P], F32R, XT0 + 40000)
        w_hi = [at(f"w_hi{i}", [128, KC, HALF], F32R, W0 + i * 32768) for i in range(2)]
        w_lo = [at(f"w_lo{i}", [128, KC, HALF], F32R, W0 + i * 32768 + 16384) for i in range(2)]
        w_raw = [at(f"w_raw{i}", [128, KC, HALF], F32, W0 + i * 32768 + 16384) for i in range(2)]
        z_hi = at("z_hi", [P, TILES, HALF], F32R, Z0)
        z_lo = at("z_lo", [P, TILES, HALF], F32R, Z0 + 20480)
        cell = at("cell", [P, TILES, HALF], F32, Z0)
        acc = at("acc", [P, TILES, DIM], F32, Z0)
        counts = at("counts", [P, (NODES + WIN) * TILES], U16, Z0)
        o = Z0 + 25504
        src_i = at("src_i", [P, CHUNKS], I32, o)
        dst_i = at("dst_i", [P, CHUNKS], I32, o + 1280)
        src_p = at("src_p", [P, CHUNKS], F32, o + 2560)
        src_b = at("src_b", [P, CHUNKS], F32, o + 3840)
        key = at("key", [P, CHUNKS], F32, o + 5120)
        gdst = at("gdst", [80, 2, 2 * P], I32, o + 6400)
        hot_p = at("hot_p", [P, UNROLL, 2, P + 3], BF16, o + 8416)
        hot_k = at("hot_k", [P, UNROLL, 2, WCOLS], BF16, o + 10464)
        assert used["hot_k"] <= S0
        exp_hi = [at(f"exp_hi{i}", [P, TILES, P], F32R, XT0 + i * 5024) for i in range(2)]
        exp_lo = [at(f"exp_lo{i}", [P, TILES, P], F32R, XT0 + 10048 + i * 5024) for i in range(2)]
        gmin = at("gmin", [80, 2], F32, XT0 + 24000)
        gspan = at("gspan", [80, 2], F32, XT0 + 24032)
        base_b = at("base_b", [P, GROUPS], F32, XT0 + 24064)
        base_r = at("base_r", [1, GROUPS], F32, XT0 + 24704)
        span_r = at("span_r", [1, GROUPS], F32, XT0 + 25344)
        addr = at("addr", [1, GROUPS], I32, XT0 + 25984)
        steps_r = at("steps_r", [1, MAX_ROUNDS], F32, XT0 + 26656)
        over_r = at("over_r", [1, MAX_ROUNDS], F32, XT0 + 26880)
        rnd = at("rnd", [1, 4], F32, XT0 + 27104)
        rnd_i = at("rnd_i", [1, 1], I32, XT0 + 27136)
        a_hi = [at(f"a_hi{i}", [P, TILES, P], F32R, S0 + i * 5024) for i in range(2)]
        a_lo = at("a_lo", [P, TILES // 2, P], F32R, S0 + 20288)
        xo = [at(f"xo{i}", [P, HALF], F32, S0 + 10048 + i * 2048) for i in range(2)]
        tmp = [at(f"tmp{i}", [P, HALF], F32, S0 + 14144 + i * 2048) for i in range(2)]
        bias = at("bias", [P, HALF], F32, S0 + 18240)
        xin = [at(f"xin{i}", [P, DIM], F32, S0 + i * 4096) for i in range(2)]
        yn = [at(f"yn{i}", [P, DIM], F32, S0 + 8192 + i * 4096) for i in range(2)]
        gw_raw = at("gw_raw", [128, KC, EXPERTS], F32, S0)
        gw_hi = at("gw_hi", [128, KC, EXPERTS], F32R, S0 + 256)
        gw_lo = at("gw_lo", [128, KC, EXPERTS], F32R, S0 + 512)
        gb = at("gb", [P, EXPERTS], F32, S0 + 768)
        lg = at("lg", [P, TILES, EXPERTS], F32, S0 + 800)
        sel = at("sel", [P, TILES, EXPERTS], F32, S0 + 1120)
        r10 = at("r10", [P, TILES], F32, S0 + 1440)
        zero10 = at("zero10", [P, TILES], F32, S0 + 1504)
        wt = at("wt", [EXPERTS, TILES, P], F32, S0 + 1568)
        eb = at("eb", [EXPERTS, DIM], F32, S0 + 16384)
        ident = at("ident", [P, P], F32, C0)
        ident_r = at("ident_r", [P, P], F32R, C0 + 512)
        ones_r = at("ones_r", [P, 2], F32R, C0 + 1024)
        iota = at("iota", [P, WCOLS], BF16, C0 + 1056)
        row_no = at("row_no", [P, 1], F32, C0 + 1568)
        deg = at("deg", [P, TILES], F32, C0 + 1600)
        dinv = at("dinv", [P, TILES], F32, C0 + 1664)
        deg_inv = at("deg_inv", [P, TILES], F32, C0 + 1728)
        dmax = at("dmax", [P, 1], F32, C0 + 1792)
        dmax_all = at("dmax_all", [P, 1], F32, C0 + 1824)
        big_i = at("big_i", [1, 1], I32, C0 + 1856)
        bn = [at(f"bn{i}", [P, 2, 6], F32, C0 + 1888 + 64 * i) for i in range(2)]
        mv = [at(f"mv{i}", [P, 2], F32, C0 + 2016 + 32 * i) for i in range(2)]
        std = [at(f"std{i}", [P, 1], F32, C0 + 2080 + 32 * i) for i in range(2)]
        rstd = [at(f"rstd{i}", [P, 1], F32, C0 + 2144 + 32 * i) for i in range(2)]
        assert used["rstd1"] <= 229368, used["rstd1"]

        ps = [ctx.enter_context(nc.psum_tensor(f"ps{i}", [128, 512], F32)) for i in range(8)]
        hist_ps = ps[RING:RING + 2]
        deg_ps = ps[7]

        ps_full = sem("ps_full")
        ps_free = sem("ps_free")
        hi_done = sem("hi_done")
        dstep = sem("dstep")
        astep = sem("astep")
        edges_in = sem("edges_in")
        stat_out = sem("stat_out")
        stat_ready = sem("stat_ready")
        stat_in = sem("stat_in")
        iota_done = sem("iota_done")
        const_done = sem("const_done")
        rounds_ready = sem("rounds_ready")
        round_step = sem("round_step")
        round_begun = sem("round_begun")
        hot_ready = sem("hot_ready")
        hist_done = sem("hist_done")
        hist_added = sem("hist_added")
        counts_ready = sem("counts_ready")
        exp_hi_done = sem("exp_hi_done")
        exp_lo_done = sem("exp_lo_done")
        exp_used = sem("exp_used")
        exp_stored = [sem(f"exp_stored{i}") for i in range(2)]
        dmax_ready = sem("dmax_ready")
        dmax_done = sem("dmax_done")
        big_ready = sem("big_ready")
        dinv_sum = sem("dinv_sum")
        dinv_root = sem("dinv_root")
        dinv_ready = sem("dinv_ready")
        w_landed = [sem(f"w_landed{i}") for i in range(2)]
        w_turn = sem("w_turn")
        w_hi_made = sem("w_hi_made")
        w_ready = sem("w_ready")
        pass_done = sem("pass_done")
        xin_landed = [sem(f"xin_landed{i}") for i in range(2)]
        acc_landed = [sem(f"acc_landed{i}") for i in range(2)]
        var_ready = sem("var_ready")
        std_ready = sem("std_ready")
        y_ready = sem("y_ready")
        a_landed = [sem(f"a_landed{i}") for i in range(2)]
        alo_landed = sem("alo_landed")
        alo_used = sem("alo_used")
        a_used = sem("a_used")
        res_landed = [sem(f"res_landed{i}") for i in range(2)]
        out_ready = sem("out_ready")
        stored = [sem(f"stored{i}") for i in range(2)]
        bias_landed = sem("bias_landed")
        bias_used = sem("bias_used")
        pre_ready = sem("pre_ready")
        gate_done = sem("gate_done")
        cell_ready = sem("cell_ready")
        tanh_done = sem("tanh_done")
        gate_in = sem("gate_in")
        gw_ready = sem("gw_ready")
        logits_done = sem("logits_done")
        shifted = sem("shifted")
        exp_done = sem("exp_done")
        weights_ready = sem("weights_ready")
        wt_done = sem("wt_done")
        wt_ready = sem("wt_ready")
        final = sem("final")

        def bank(j):
            return ps[j % RING]

        class Steps:

            def __init__(self, eng, s):
                self.eng, self.sem, self.at = eng, s, 0

            def __call__(self, ins):
                ins.then_inc(self.sem, 1)
                self.at = self.at + 1
                self.eng.wait_ge(self.sem, self.at)

        block = ctx.enter_context(nc.Block())

        STAGE_IO = [(x_t, x1_t), (x1_t, x2_t), (None, h1_t), (x2_t, x3_t)]

        @block.sync
        def _(sp):
            sp.dma_start(src_i[:], src_c).then_inc(edges_in, 16)
            sp.dma_start(dst_i[:], dst_c).then_inc(edges_in, 16)
            sp.dma_start(gdst[:], dst_g).then_inc(edges_in, 16)
            sp.wait_ge(stat_ready, 1)
            with nc.allow_non_contiguous_dma(reason="160 numbers"):
                for i, t in enumerate((gmin, gspan)):
                    sp.dma_start(stat_d[i].rearrange("(a g) -> g a", a=2), t[:]).then_inc(stat_out, 16)
            sp.wait_ge(stat_out, 32)
            sp.dma_start(base_b[:], stat_d[0].partition_broadcast(P)).then_inc(stat_in, 16)
            sp.dma_start(base_r[:], stat_d[0:1, :]).then_inc(stat_in, 16)
            sp.dma_start(span_r[:], stat_d[1:2, :]).then_inc(stat_in, 16)
            for t in range(TILES):
                sp.wait_ge(exp_hi_done, t + 1)
                sp.dma_start(ahi_d[t], exp_hi[t % 2][:].rearrange("p b d -> p (b d)").bitcast(F32)).then_inc(exp_stored[t % 2], 16)
                sp.wait_ge(exp_lo_done, t + 1)
                sp.dma_start(alo_d[t], exp_lo[t % 2][:].rearrange("p b d -> p (b d)").bitcast(F32)).then_inc(exp_stored[t % 2], 16)
            for i in range(2):
                sp.wait_ge(exp_stored[i], 16 * TILES)
            sp.wait_ge(big_ready, 1)
            big = sp.value_load(big_i[:], min_val=0, max_val=1)

            def prep_loads(s, source, normed):
                for t in range(TILES):
                    n = (s * TILES + t)
                    if s == 4:
                        if t >= 2:
                            sp.wait_ge(var_ready, 3 * TILES + t - 1)
                        sp.dma_start(acc[:, t, :], source[t]).then_inc(acc_landed[t % 2], 16)
                        continue
                    if t >= 2:
                        if normed:
                            sp.wait_ge(y_ready, (s if s < 3 else s - 1) * TILES + t - 1)
                        else:
                            sp.wait_ge(ps_full, J_PREP[s] + 2 * (t - 1))
                    sp.dma_start(xin[t % 2][:], source[t]).then_inc(xin_landed[t % 2], 16)

            def stage_end(s, j):
                sp.wait_ge(ps_free, j)
                for i in range(2):
                    sp.wait_ge(stored[i], 16 * TILES * (s + 1))

            def load_a(a, t):
                if a is not None:
                    sp.wait_ge(a_used, a)
                sp.dma_start(a_hi[t % 2][:].rearrange("p b d -> p (b d)").bitcast(F32), ahi_d[t]).then_inc(a_landed[t % 2], 16)

            def load_a_lo(n, t):
                with sp.If(big > 0):
                    for part in range(2):
                        sp.wait_ge(alo_used, n + part)
                        sp.dma_start(a_lo[:].rearrange("p b d -> p (b d)").bitcast(F32),
                                     alo_d[t][:, part * 625:(part + 1) * 625]).then_inc(alo_landed, 16)

            def load_bias(m, b, h):
                if m is not None:
                    sp.wait_ge(bias_used, m)
                sp.dma_start(bias[:], b[bass.ds(h * HALF, HALF)].partition_broadcast(P)).then_inc(bias_landed, 16)

            def load_res(u, source, t, h):
                if u is not None:
                    sp.wait_ge(stored[t % 2], u)
                sp.dma_start(xo[t % 2][:], source[t][:, bass.ds(h * HALF, HALF)]).then_inc(res_landed[t % 2], 16)

            def store(u, target, t, h):
                sp.wait_ge(out_ready, u)
                sp.dma_start(target[t][:, bass.ds(h * HALF, HALF)], xo[t % 2][:]).then_inc(stored[t % 2], 16)

            prep_loads(0, x_t, True)
            sp.wait_ge(ps_free, J_GCN)
            for h in range(HALVES):
                load_bias(h or None, gcn_b, h)
                for t in range(TILES):
                    u = h * TILES + t
                    load_a(u - 1 if u >= 2 else None, t)
                    load_a_lo(2 * u, t)
                    load_res(16 * (u // 2) if u >= 2 else None, x_t, t, h)
                    if t:
                        store(u, x1_t, t - 1, h)
                store(u + 1, x1_t, TILES - 1, h)
            stage_end(0, J_PREP[1])
            prep_loads(1, x1_t, True)
            sp.wait_ge(ps_free, J_LSTM)
            for h in range(HALVES):
                for g in range(3):
                    load_bias(2 + 3 * h + g, lstm_b[g], h)
                for t in range(TILES):
                    u = 20 + h * TILES + t
                    load_res(16 * (u // 2), x1_t, t, h)
                    if t:
                        store(u, x2_t, t - 1, h)
                store(u + 1, x2_t, TILES - 1, h)
            stage_end(1, J_PREP[2])
            for layer in range(SAGE_LAYERS):
                s = 2 + layer
                prep_loads(s, x2_t if layer == 0 else h1_t, layer == 0)
                sp.wait_ge(ps_free, J_SAGE[layer])
                with sp.Fori(0, HALVES) as h:
                    load_bias(8 + 2 * layer + h, sage_b[layer], h)
                    for t in range(TILES):
                        u = 20 * s + h * TILES + t
                        load_a(20 * (1 + layer) + h * TILES + t - 1, t)
                        load_a_lo(2 * (20 * (1 + layer) + h * TILES + t), t)
                        u2 = 16 * (10 * s + t // 2) + h * (8 * TILES)
                        if layer == 1:
                            load_res(u2, x2_t, t, h)
                        if t:
                            store(u, (h1_t, x3_t)[layer], t - 1, h)
                    store(u + 1, (h1_t, x3_t)[layer], TILES - 1, h)
                stage_end(s, J_PREP[s + 1])
            sp.dma_start(gw_raw[:], gate_w.rearrange("(k p) e -> p k e", p=128)).then_inc(gate_in, 16)
            sp.dma_start(gb[:], gate_b.partition_broadcast(P)).then_inc(gate_in, 16)
            sp.dma_start(eb[:], expert_b).then_inc(gate_in, 16)
            prep_loads(4, x3_t, True)
            for t in range(TILES):
                sp.wait_ge(ps_free, J_END - TILES + t + 1)
                sp.dma_start(out_t[t], acc[:, t, :]).then_inc(final, 16)
            sp.wait_ge(final, 16 * TILES)

        @block.gpsimd
        def _(pool):
            nc.gpsimd.iota(iota[:], [[1, WCOLS]], base=0, channel_multiplier=0,
                           allow_small_or_imprecise_dtypes=True).then_inc(iota_done, 1)
            nc.gpsimd.iota(row_no[:], [[0, 1]], base=0, channel_multiplier=1,
                           allow_small_or_imprecise_dtypes=True).then_inc(iota_done, 1)
            nc.gpsimd.iota(steps_r[:], [[WIN, MAX_ROUNDS]], base=WIN, channel_multiplier=0,
                           allow_small_or_imprecise_dtypes=True).then_inc(iota_done, 1)

            def weights(n, n_last, source):
                i = n_last % 2
                if not (isinstance(n, int) and n < 2):
                    pool.wait_ge(pass_done, n - 1)
                    pool.sem_inc(w_turn, 1)
                pool.dma_start(w_raw[i][:], source).then_inc(w_landed[i], 16)

            def split(n, i, landed):
                pool.wait_ge(w_landed[i], landed)
                pool.sem_inc(w_turn, 1)
                nc.gpsimd.tensor_copy(w_hi[i][:], w_raw[i][:]).then_inc(w_hi_made, 1)
                pool.wait_ge(w_hi_made, n + 1)
                nc.gpsimd.tensor_tensor(out=w_lo[i][:], in0=w_raw[i][:], in1=w_hi[i][:].bitcast(F32),
                                        op=ALU.subtract).then_inc(w_ready, 1)

            def half(w, h):
                return w[:, bass.ds(h * HALF, HALF)].rearrange("(k p) n -> p k n", p=128)

            fixed = [half(gcn_w, h) for h in range(HALVES)]
            fixed += [half(lstm_w[g], h) for h in range(HALVES) for g in range(3)]
            for n, source in enumerate(fixed):
                weights(n, n, source)
                split(n, n % 2, 16 * (n // 2 + 1))
                if n == 0:
                    pool.wait_ge(dmax_ready, 1)
                    nc.gpsimd.partition_all_reduce(dmax_all[:], dmax[:], P, bass.bass_isa.ReduceOp.max).then_inc(dmax_done, 1)
            for layer in range(SAGE_LAYERS):
                with pool.Fori(0, HALVES) as h:
                    for i, w in enumerate((sage_wn[layer], sage_ws[layer])):
                        n = N_SAGE[layer] + 2 * h + i
                        weights(n, i, half(w, h))
                        split(n, i, 16 * (N_SAGE[layer] // 2 + 1) + 16 * h)
            with pool.Fori(0, EXPERTS) as e:
                for h in range(HALVES):
                    n = N_MOE + 2 * e + h
                    source = expert_w[bass.ds(e, 1), :, h * HALF:(h + 1) * HALF].rearrange(
                        "e (k p) n -> p (e k) n", p=128)
                    weights(n, h, source)
                    split(n, h, 16 * (N_MOE // 2 + 1) + 16 * e)

        @block.scalar
        def _(act):
            for t in range(TILES):
                if t == 0:
                    act.wait_ge(counts_ready, 1)
                if t >= 2:
                    act.wait_ge(exp_used, t - 1)
                    act.wait_ge(exp_stored[t % 2], 32 * (t // 2))
                act.activation(exp_hi[t % 2][:],
                               counts[:, t * P * TILES:(t + 1) * P * TILES].rearrange("p (d b) -> p b d", b=TILES),
                               ACT.Copy).then_inc(exp_hi_done, 1)
            act.wait_ge(dinv_sum, 1)
            act.activation(deg[:], dinv[:], ACT.Sqrt).then_inc(dinv_root, 1)

            def prep(s, normed):
                sn = s if s < 3 else s - 1
                if s:
                    act.wait_ge(ps_free, J_PREP[s])

                def root(t):
                    act.wait_ge(var_ready, sn * TILES + t + 1)
                    act.activation(std[t % 2][:], mv[t % 2][:, 1:2], ACT.Sqrt).then_inc(std_ready, 1)

                def highs(t):
                    for g in range(2):
                        j = J_PREP[s] + 2 * t + g
                        act.wait_ge(ps_full, j + 1)
                        act.activation(xt_hi[:, t, 4 * g:4 * g + 4, :].rearrange("p k n -> p (k n)"),
                                       bank(j)[:, 0:4 * P], ACT.Copy).then_inc(hi_done, 1)
                for t in range(TILES):
                    if normed:
                        root(t)
                    if t:
                        highs(t - 1)
                highs(TILES - 1)

            def z_highs(j0, scale):
                for t in range(TILES):
                    act.wait_ge(ps_full, j0 + t + 1)
                    act.activation(z_hi[:, t, :], ps[t % RING][0:P, :], ACT.Copy,
                                   scale=dinv[:, t:t + 1] if scale else 1.0).then_inc(hi_done, 1)

            prep(0, True)
            act.wait_ge(dinv_ready, 1)
            for h in range(HALVES):
                z_highs(J_GCN + 20 * h, True)
                act.wait_ge(ps_free, J_GCN + 20 * h + 20)
            prep(1, True)
            for h in range(HALVES):
                for g in range(3):
                    for t in range(TILES):
                        n = 30 * h + 10 * g + t
                        act.wait_ge(pre_ready, n + 1)
                        if g == 0:
                            act.activation(cell[:, t, :], tmp[t % 2][:], ACT.Sigmoid).then_inc(gate_done, 1)
                        else:
                            act.activation(tmp[t % 2][:], tmp[t % 2][:], ACT.Tanh if g == 1 else ACT.Sigmoid).then_inc(gate_done, 1)
                        if g == 1:
                            act.wait_ge(cell_ready, 10 * h + t + 1)
                            act.activation(cell[:, t, :], cell[:, t, :], ACT.Tanh).then_inc(tanh_done, 1)
                act.wait_ge(out_ready, 20 + 10 * (h + 1))
            for layer in range(SAGE_LAYERS):
                prep(2 + layer, layer == 0)
                with act.Fori(0, HALVES) as h:
                    z_highs(J_SAGE[layer] + 30 * h, False)
                    act.wait_ge(ps_free, J_SAGE[layer] + 30 * h + 30)
            prep(4, True)
            act.wait_ge(shifted, 1)
            act.activation(lg[:], lg[:], ACT.Exp).then_inc(exp_done, 1)
            for b in range(3):
                act.wait_ge(wt_done, b + 1)
                n = min(4, TILES - 4 * b)
                act.activation(wt[:, 4 * b:4 * b + n, :].rearrange("e t p -> e (t p)"),
                               ps[RING + b][0:EXPERTS, 0:n * P], ACT.Copy).then_inc(wt_ready, 1)

        @block.vector
        def _(dve):
            step = Steps(dve, dstep)
            V = nc.vector
            dve.wait_ge(iota_done, 3)
            V.tensor_scalar(ident[:], iota[:, 0:P], row_no[:], None, ALU.is_equal).then_inc(const_done, 1)
            V.tensor_scalar(ident_r[:], iota[:, 0:P], row_no[:], None, ALU.is_equal).then_inc(const_done, 1)
            V.memset(ones_r[:].bitcast(F32), 1.0).then_inc(const_done, 1)
            V.memset(counts[:].bitcast(I32), 0)
            dve.wait_ge(edges_in, 48)
            V.tensor_reduce(gmin[:], gdst[:], AX.X, ALU.min)
            step(V.tensor_reduce(gspan[:], gdst[:], AX.X, ALU.max))
            step(V.tensor_tensor(gspan[:], gspan[:], gmin[:], ALU.subtract))
            dve.sem_inc(stat_ready, 1)
            step(V.tensor_copy(src_p[:], src_i[:]))
            step(V.tensor_scalar(src_b[:], src_p[:], float(P), None, ALU.is_ge))
            for b in range(2, TILES):
                step(V.scalar_tensor_tensor(src_b[:], src_p[:], float(P * b), src_b[:], ALU.is_ge, ALU.add))
            V.scalar_tensor_tensor(src_p[:], src_b[:], float(-P), src_p[:], ALU.mult, ALU.add)
            step(V.tensor_copy(key[:], dst_i[:]))
            step(V.scalar_tensor_tensor(key[:], key[:], float(TILES), src_b[:], ALU.mult, ALU.add))
            dve.wait_ge(stat_in, 48)
            step(V.scalar_tensor_tensor(
                key[:].rearrange("p (g c) -> p g c", c=2), base_b[:].unsqueeze(2).to_broadcast([P, GROUPS, 2]),
                float(-TILES), key[:].rearrange("p (g c) -> p g c", c=2), ALU.mult, ALU.add))
            step(V.reduce_max(rnd[:, 0:1], span_r[:], AX.X))
            step(V.tensor_scalar(over_r[:], steps_r[:], rnd[:, 0:1], 1.0, ALU.is_le, ALU.add, accum_out=rnd[:, 1:2]))
            step(V.tensor_copy(rnd_i[:], rnd[:, 1:2]))
            dve.sem_inc(hist_added, 1)
            dve.sem_inc(hist_added, 1)
            dve.sem_inc(rounds_ready, 1)
            rounds = dve.value_load(rnd_i[:], min_val=1, max_val=MAX_ROUNDS)
            rstep = Steps(dve, round_step)
            with dve.Fori(0, rounds) as r:
                rstep.at = r * 3
                rstep(V.tensor_scalar(addr[:], base_r[:], float(NODES), float(TILES), ALU.min, ALU.mult))
                dve.sem_inc(round_begun, 1)
                with dve.Fori(0, GROUPS // UNROLL) as it:
                    starts = [dve.value_load(addr[0:1, bass.ds(it * UNROLL + q, 1)], min_val=0, max_val=NODES * TILES)
                              for q in range(UNROLL)]
                    done = (r * (GROUPS // UNROLL) + it) * UNROLL

                    def hots(q):
                        for c in range(2):
                            col = bass.ds(it * (2 * UNROLL) + 2 * q + c, 1)
                            V.tensor_scalar(hot_p[:, q, c, 0:P], iota[:, 0:P], src_p[:, col], None, ALU.is_equal)
                            last = V.tensor_scalar(hot_k[:, q, c, :], iota[:], key[:, col], None, ALU.is_equal)
                        last.then_inc(hot_ready, 1)

                    def add(q):
                        dve.wait_ge(hist_done, done + q + 1)
                        dve.wait_ge(hist_added, done + q + 2)
                        win = counts[:, bass.ds(starts[q], WCOLS)]
                        V.tensor_tensor(out=win, in0=hist_ps[q % 2][0:P, 0:WCOLS], in1=win, op=ALU.add).then_inc(hist_added, 1)

                    hots(0)
                    hots(1)
                    add(0)
                    hots(2)
                    add(1)
                    hots(3)
                    add(2)
                    add(3)
                rstep(V.tensor_scalar(key[:], key[:], float(-WCOLS), None, ALU.add))
                rstep(V.tensor_scalar(base_r[:], base_r[:], float(WIN), None, ALU.add))
            dve.wait_ge(hist_added, rounds * GROUPS + 2)
            dve.sem_inc(counts_ready, 1)
            for t in range(TILES):
                dve.wait_ge(exp_hi_done, t + 1)
                if t >= 2:
                    dve.wait_ge(exp_used, t - 1)
                    dve.wait_ge(exp_stored[t % 2], 32 * (t // 2))
                V.tensor_tensor(out=exp_lo[t % 2][:],
                                in0=counts[:, t * P * TILES:(t + 1) * P * TILES].rearrange("p (d b) -> p b d", b=TILES),
                                in1=exp_hi[t % 2][:].bitcast(F32), op=ALU.subtract).then_inc(exp_lo_done, 1)
            dve.wait_ge(exp_used, TILES)
            V.tensor_reduce(dmax[:], deg_ps[0:P, 0:2 * TILES], AX.X, ALU.max).then_inc(dmax_ready, 1)
            step(V.tensor_scalar(deg_inv[:], deg_ps[0:P, 0:2 * TILES:2], 1.0, None, ALU.max))
            V.reciprocal(deg_inv[:], deg_inv[:])
            V.tensor_scalar(dinv[:], deg_ps[0:P, 0:2 * TILES:2], 1.0, None, ALU.add).then_inc(dinv_sum, 1)
            dve.wait_ge(dmax_done, 1)
            V.tensor_scalar(big_i[:], dmax_all[0:1, :], float(EXACT), None, ALU.is_gt).then_inc(big_ready, 1)
            dve.wait_ge(dinv_root, 1)
            V.reciprocal(dinv[:], deg[:]).then_inc(dinv_ready, 1)

            def prep(s, normed):
                sn = s if s < 3 else s - 1
                if s:
                    dve.wait_ge(ps_free, J_PREP[s])

                def tile(t):
                    return acc[:, t, :] if s == 4 else xin[t % 2][:]

                def stats(t):
                    i = t % 2
                    if s == 4:
                        dve.wait_ge(acc_landed[i], 16 * (t // 2 + 1))
                    else:
                        dve.wait_ge(xin_landed[i], 16 * (s * TILES // 2 + t // 2 + 1))
                    V.bn_stats(bn[i][:, 0, :], tile(t)[:, 0:HALF])
                    step(V.bn_stats(bn[i][:, 1, :], tile(t)[:, HALF:DIM]))
                    step(V.bn_aggr(mv[i][:], bn[i][:].rearrange("p a b -> p (a b)")))
                    V.tensor_scalar(mv[i][:, 1:2], mv[i][:, 1:2], LN_EPS, None, ALU.add).then_inc(var_ready, 1)

                def norm(t):
                    i = t % 2
                    dve.wait_ge(std_ready, sn * TILES + t + 1)
                    step(V.reciprocal(rstd[i][:], std[i][:]))
                    if t >= 2:
                        dve.wait_ge(ps_full, J_PREP[s] + 2 * (t - 1))
                    V.tensor_scalar(yn[i][:], tile(t), mv[i][:, 0:1], rstd[i][:], ALU.subtract, ALU.mult).then_inc(y_ready, 1)

                def lows(t):
                    for g in range(2):
                        j = J_PREP[s] + 2 * t + g
                        hi = xt_hi[:, t, 4 * g:4 * g + 4, :].rearrange("p k n -> p (k n)")
                        dve.wait_ge(hi_done, hi_base[0] + 2 * t + g + 1)
                        V.tensor_tensor(out=xt_lo[:, t, 4 * g:4 * g + 4, :].rearrange("p k n -> p (k n)"),
                                        in0=bank(j)[:, 0:4 * P], in1=hi.bitcast(F32), op=ALU.subtract).then_inc(ps_free, 1)
                for t in range(TILES + 2):
                    if normed and t < TILES:
                        stats(t)
                    if normed and 1 <= t <= TILES:
                        norm(t - 1)
                    if t >= 2:
                        lows(t - 2)
                hi_base[0] += 2 * TILES

            def z_lows(j0, hi0, scale):
                for t in range(TILES):
                    dve.wait_ge(hi_done, hi0 + t + 1)
                    hi = z_hi[:, t, :].bitcast(F32)
                    if scale:
                        last = V.scalar_tensor_tensor(z_lo[:, t, :], ps[t % RING][0:P, :], dinv[:, t:t + 1], hi,
                                                      ALU.mult, ALU.subtract)
                    else:
                        last = V.tensor_tensor(out=z_lo[:, t, :], in0=ps[t % RING][0:P, :], in1=hi, op=ALU.subtract)
                    last.then_inc(ps_free, 1)

            hi_base = [0]
            prep(0, True)
            dve.wait_ge(dinv_ready, 1)
            for h in range(HALVES):
                j0 = J_GCN + 20 * h
                z_lows(j0, hi_base[0], True)
                hi_base[0] += TILES
                dve.wait_ge(bias_landed, 16 * (h + 1))
                for t in range(TILES):
                    u = 10 * h + t
                    dve.wait_ge(ps_full, j0 + TILES + t + 1)
                    last = V.scalar_tensor_tensor(tmp[t % 2][:], bank(j0 + TILES + t)[0:P, :], dinv[:, t:t + 1],
                                                  bias[:], ALU.mult, ALU.add)
                    last.then_inc(ps_free, 1)
                    dve.wait_ge(ps_free, j0 + TILES + t + 1)
                    dve.wait_ge(res_landed[t % 2], 16 * (5 * h + t // 2 + 1))
                    V.scalar_tensor_tensor(xo[t % 2][:], tmp[t % 2][:], 0.0, xo[t % 2][:], ALU.max, ALU.add).then_inc(out_ready, 1)
                dve.sem_inc(bias_used, 1)
            prep(1, True)
            for h in range(HALVES):
                for g in range(3):
                    m = 2 + 3 * h + g
                    dve.wait_ge(bias_landed, 16 * (m + 1))
                    for t in range(TILES):
                        j = J_LSTM + 30 * h + 10 * g + t
                        n = 30 * h + 10 * g + t
                        dve.wait_ge(ps_full, j + 1)
                        if n >= 2:
                            dve.wait_ge(gate_done, n - 1)
                        V.tensor_tensor(out=tmp[t % 2][:], in0=bank(j)[0:P, :], in1=bias[:], op=ALU.add).then_inc(ps_free, 1)
                        dve.wait_ge(ps_free, j + 1)
                        dve.sem_inc(pre_ready, 1)
                        if g == 1:
                            dve.wait_ge(gate_done, n + 1)
                            V.tensor_tensor(out=cell[:, t, :], in0=cell[:, t, :], in1=tmp[t % 2][:], op=ALU.mult).then_inc(cell_ready, 1)
                        if g == 2:
                            dve.wait_ge(gate_done, n + 1)
                            dve.wait_ge(tanh_done, 10 * h + t + 1)
                            step(V.tensor_tensor(out=tmp[t % 2][:], in0=tmp[t % 2][:], in1=cell[:, t, :], op=ALU.mult))
                            dve.wait_ge(res_landed[t % 2], 16 * (10 + 5 * h + t // 2 + 1))
                            V.tensor_tensor(out=xo[t % 2][:], in0=tmp[t % 2][:], in1=xo[t % 2][:], op=ALU.add).then_inc(out_ready, 1)
                    dve.sem_inc(bias_used, 1)
            for layer in range(SAGE_LAYERS):
                s = 2 + layer
                prep(s, layer == 0)
                start = step.at
                hi0 = hi_base[0]
                with dve.Fori(0, HALVES) as h:
                    step.at = start + h * TILES
                    j0 = J_SAGE[layer] + 30 * h
                    z_lows(j0, hi0 + h * TILES, False)
                    dve.wait_ge(bias_landed, 16 * (8 + 2 * layer + 1) + 16 * h)
                    for t in range(TILES):
                        agg, own = (ps[(2 * t + i) % RING][0:P, :] for i in range(2))
                        ja = j0 + TILES + 2 * t
                        dve.wait_ge(ps_full, ja + 1)
                        V.scalar_tensor_tensor(tmp[t % 2][:], agg, deg_inv[:, t:t + 1], bias[:], ALU.mult, ALU.add).then_inc(ps_free, 1)
                        dve.wait_ge(ps_free, ja + 1)
                        dve.wait_ge(ps_full, ja + 2)
                        V.tensor_tensor(out=tmp[t % 2][:], in0=own, in1=tmp[t % 2][:], op=ALU.add).then_inc(ps_free, 1)
                        dve.wait_ge(ps_free, ja + 2)
                        if layer == 0:
                            dve.wait_ge(stored[t % 2], 16 * (10 * s + t // 2) + h * (8 * TILES))
                            V.tensor_scalar(xo[t % 2][:], tmp[t % 2][:], 0.0, None, ALU.max).then_inc(out_ready, 1)
                        else:
                            dve.wait_ge(res_landed[t % 2], 16 * (20 + t // 2 + 1) + h * (8 * TILES))
                            V.tensor_tensor(out=xo[t % 2][:], in0=tmp[t % 2][:], in1=xo[t % 2][:], op=ALU.add).then_inc(out_ready, 1)
                    step.at = start + h * TILES + TILES
                    dve.sem_inc(bias_used, 1)
                step.at = start
                hi_base[0] = hi0 + HALVES * TILES
            dve.wait_ge(gate_in, 48)
            dve.wait_ge(ps_free, J_PREP[4])
            step(V.tensor_copy(gw_hi[:], gw_raw[:]))
            V.tensor_tensor(out=gw_lo[:], in0=gw_raw[:], in1=gw_hi[:].bitcast(F32), op=ALU.subtract).then_inc(gw_ready, 1)
            prep(4, True)
            shape = [P, TILES, EXPERTS]
            dve.wait_ge(logits_done, 1)
            step(V.tensor_tensor(out=lg[:], in0=ps[RING][0:P, 0:TILES * EXPERTS].rearrange("p (t e) -> p t e", e=EXPERTS),
                                 in1=gb[:].unsqueeze(1).to_broadcast(shape), op=ALU.add))
            step(V.reduce_max(r10[:], lg[:], AX.X))
            V.tensor_tensor(out=lg[:], in0=lg[:], in1=r10[:].unsqueeze(2).to_broadcast(shape), op=ALU.subtract).then_inc(shifted, 1)
            dve.wait_ge(exp_done, 1)
            step(V.reduce_sum(r10[:], lg[:], AX.X))
            step(V.reciprocal(r10[:], r10[:]))
            step(V.tensor_tensor(out=lg[:], in0=lg[:], in1=r10[:].unsqueeze(2).to_broadcast(shape), op=ALU.mult))
            step(V.tensor_scalar(sel[:], lg[:], THRESHOLD, None, ALU.is_ge))
            step(V.tensor_tensor(out=lg[:], in0=lg[:], in1=sel[:], op=ALU.mult))
            step(V.reduce_sum(r10[:], lg[:], AX.X))
            step(V.tensor_scalar(zero10[:], r10[:], 0.0, None, ALU.is_equal))
            step(V.tensor_tensor(out=r10[:], in0=r10[:], in1=zero10[:], op=ALU.add))
            step(V.reciprocal(r10[:], r10[:]))
            step(V.tensor_tensor(out=lg[:], in0=lg[:], in1=r10[:].unsqueeze(2).to_broadcast(shape), op=ALU.mult))
            dve.sem_inc(weights_ready, 1)
            for h in range(HALVES):
                for t in range(TILES):
                    j = J_EXPERT_B + h * TILES + t
                    dve.wait_ge(ps_full, j + 1)
                    part = acc[:, t, h * HALF:(h + 1) * HALF]
                    V.tensor_tensor(out=part, in0=bank(j)[0:P, :], in1=part, op=ALU.add).then_inc(ps_free, 1)
            with dve.Fori(0, EXPERTS) as e:
                for h in range(HALVES):
                    for t in range(TILES):
                        n = h * TILES + t
                        j = J_EXPERT + 2 * TILES * e + n
                        dve.wait_ge(ps_full, j + 1)
                        dve.wait_ge(ps_free, j - 2 * TILES + 1)
                        part = acc[:, t, h * HALF:(h + 1) * HALF]
                        V.scalar_tensor_tensor(part, ps[n % RING][0:P, :], lg[:, t, bass.ds(e, 1)], part,
                                               ALU.mult, ALU.add).then_inc(ps_free, 1)

        @block.tensor
        def _(pe):
            mm = nc.tensor.matmul
            pe.wait_ge(const_done, 3)
            pe.wait_ge(rounds_ready, 1)
            rounds = pe.value_load(rnd_i[:], min_val=1, max_val=MAX_ROUNDS)
            with pe.Fori(0, rounds) as r:
                with pe.Fori(0, GROUPS // UNROLL) as it:
                    done = (r * (GROUPS // UNROLL) + it) * UNROLL
                    for q in range(UNROLL):
                        pe.wait_ge(hot_ready, done + q + 1)
                        pe.wait_ge(hist_added, done + q + 1)
                        for c in range(2):
                            last = mm(hist_ps[q % 2][0:P, 0:WCOLS], hot_p[:, q, c, 0:P], hot_k[:, q, c, :],
                                      start=c == 0, stop=c == 1)
                        last.then_inc(hist_done, 1)
            for t in range(TILES):
                pe.wait_ge(exp_hi_done, t + 1)
                pe.wait_ge(exp_lo_done, t + 1)
                for n in range(2 * TILES):
                    part = (exp_hi, exp_lo)[n // TILES][t % 2]
                    last = mm(deg_ps[0:P, 2 * t:2 * t + 2], part[:, n % TILES, :], ones_r[:],
                              start=n == 0, stop=n == 2 * TILES - 1)
                last.then_inc(exp_used, 1)
            pe.wait_ge(big_ready, 1)
            big = pe.value_load(big_i[:], min_val=0, max_val=1)

            def free(j):
                if not (isinstance(j, int) and j < RING):
                    pe.wait_ge(ps_free, j - RING + 1)

            def prep(s, normed):
                sn = s if s < 3 else s - 1
                for t in range(TILES):
                    if normed:
                        pe.wait_ge(y_ready, sn * TILES + t + 1)
                        y = yn[t % 2]
                    else:
                        pe.wait_ge(xin_landed[t % 2], 16 * (s * TILES // 2 + t // 2 + 1))
                        y = xin[t % 2]
                    for g in range(2):
                        j = J_PREP[s] + 2 * t + g
                        free(j)
                        for k in range(4):
                            c = 4 * g + k
                            last = nc.tensor.transpose(bank(j)[:, k * P:(k + 1) * P], y[:, c * 128:(c + 1) * 128], ident[:])
                        last.then_inc(ps_full, 1)

            PARTS = ((xt_hi, 0), (xt_hi, 1), (xt_lo, 0))

            def product(dst, t, arena):
                w = (w_hi[arena], w_lo[arena])
                for k in range(KC):
                    for n, (xt, i) in enumerate(PARTS):
                        last = mm(dst[0:P, :], xt[:, t, k, :], w[i][:, k, :],
                                  start=k == 0 and n == 0, stop=k == KC - 1 and n == 2)
                return last

            def xt_ready(s):
                pe.wait_ge(ps_free, J_PREP[s] + 2 * TILES)

            def z_pass(j0, n, arena):
                pe.wait_ge(w_ready, n + 1)
                for t in range(TILES):
                    free(j0 + t)
                    last = product(ps[t % RING], t, arena)
                    last.then_inc(ps_full, 1)
                pe.wait_ge(ps_full, j0 + TILES)
                nc.tensor.sem_inc(pass_done, 1)
                pe.wait_ge(ps_free, j0 + TILES)

            def aggregate(dst, t, a, landed, own):
                pe.wait_ge(a_landed[t % 2], landed)
                for b in range(TILES):
                    mm(dst[0:P, :], a_hi[t % 2][:, b, :], z_hi[:, b, :], start=b == 0, stop=False)
                    if b < TILES - 1:
                        mm(dst[0:P, :], a_hi[t % 2][:, b, :], z_lo[:, b, :], start=False, stop=False)
                if own:
                    mm(dst[0:P, :], ident_r[:], z_hi[:, t, :], start=False, stop=False)
                    mm(dst[0:P, :], ident_r[:], z_lo[:, t, :], start=False, stop=False)
                with pe.If(big > 0):
                    for part in range(2):
                        pe.wait_ge(alo_landed, 32 * a + 16 * (part + 1))
                        for b in range(TILES // 2):
                            last = mm(dst[0:P, :], a_lo[:, b, :], z_hi[:, part * (TILES // 2) + b, :], start=False, stop=False)
                        last.then_inc(alo_used, 1)
                last = mm(dst[0:P, :], a_hi[t % 2][:, TILES - 1, :], z_lo[:, TILES - 1, :], start=False, stop=True)
                last.then_inc(ps_full, 1)

            prep(0, True)
            xt_ready(0)
            for h in range(HALVES):
                j0 = J_GCN + 20 * h
                z_pass(j0, N_GCN + h, h)
                for t in range(TILES):
                    j = j0 + TILES + t
                    free(j)
                    aggregate(bank(j), t, 10 * h + t, 16 * (5 * h + t // 2 + 1), True)
                    pe.wait_ge(ps_full, j + 1)
                    nc.tensor.sem_inc(a_used, 1)
            prep(1, True)
            xt_ready(1)
            for h in range(HALVES):
                for g in range(3):
                    n = N_LSTM + 3 * h + g
                    pe.wait_ge(w_ready, n + 1)
                    for t in range(TILES):
                        j = J_LSTM + 30 * h + 10 * g + t
                        free(j)
                        product(bank(j), t, n % 2).then_inc(ps_full, 1)
                    pe.wait_ge(ps_full, j + 1)
                    nc.tensor.sem_inc(pass_done, 1)
            for layer in range(SAGE_LAYERS):
                s = 2 + layer
                prep(s, layer == 0)
                xt_ready(s)
                with pe.Fori(0, HALVES) as h:
                    j0 = J_SAGE[layer] + 30 * h
                    n = N_SAGE[layer] + 2 * h
                    z_pass(j0, n, 0)
                    pe.wait_ge(w_ready, n + 2)
                    for t in range(TILES):
                        ja = j0 + TILES + 2 * t
                        free(ja)
                        aggregate(ps[(2 * t) % RING], t, 20 * (1 + layer) + h * TILES + t,
                                  16 * (10 * (1 + layer) + t // 2 + 1) + h * (8 * TILES), False)
                        free(ja + 1)
                        product(ps[(2 * t + 1) % RING], t, 1).then_inc(ps_full, 1)
                        pe.wait_ge(ps_full, ja + 1)
                        nc.tensor.sem_inc(a_used, 1)
                    pe.wait_ge(ps_full, j0 + 30)
                    nc.tensor.sem_inc(pass_done, 1)
            prep(4, True)
            xt_ready(4)
            pe.wait_ge(gw_ready, 1)
            for t in range(TILES):
                for k in range(KC):
                    for n, (xt, i) in enumerate(PARTS):
                        last = mm(ps[RING][0:P, t * EXPERTS:(t + 1) * EXPERTS], xt[:, t, k, :], (gw_hi, gw_lo)[i][:, k, :],
                                  start=k == 0 and n == 0, stop=k == KC - 1 and n == 2)
            last.then_inc(logits_done, 1)
            pe.wait_ge(weights_ready, 1)
            for b in range(3):
                for t in range(4 * b, min(4 * b + 4, TILES)):
                    last = nc.tensor.transpose(ps[RING + b][0:EXPERTS, (t - 4 * b) * P:(t - 4 * b + 1) * P], lg[:, t, :], ident[:])
                last.then_inc(wt_done, 1)
            pe.wait_ge(wt_ready, 3)
            for h in range(HALVES):
                for t in range(TILES):
                    j = J_EXPERT_B + h * TILES + t
                    free(j)
                    mm(bank(j)[0:P, :], wt[:, t, :], eb[:, h * HALF:(h + 1) * HALF], start=True, stop=True).then_inc(ps_full, 1)
            with pe.Fori(0, EXPERTS) as e:
                for h in range(HALVES):
                    pe.wait_ge(w_ready, N_MOE + 2 * e + h + 1)
                    for t in range(TILES):
                        n = h * TILES + t
                        j = J_EXPERT + 2 * TILES * e + n
                        free(j)
                        product(ps[n % RING], t, h).then_inc(ps_full, 1)
                    pe.wait_ge(ps_full, j + 1)
                    nc.tensor.sem_inc(pass_done, 1)


def kernel(x, src, dst, L0_gnn_W, L0_gnn_b, L0_ffn_W_f, L0_ffn_b_f, L0_ffn_W_i, L0_ffn_b_i, L0_ffn_W_o,
           L0_ffn_b_o, L0_ffn_W_c, L0_ffn_b_c, L1_gnn_W_self0, L1_gnn_W_neigh0, L1_gnn_b0, L1_gnn_W_self1,
           L1_gnn_W_neigh1, L1_gnn_b1, L1_ffn_gate_w, L1_ffn_gate_b, L1_ffn_expert_w, L1_ffn_expert_b):
    import numpy as np
    import concourse.bacc as bacc
    from concourse.bass_utils import run_bass_kernel_spmd

    nc = bacc.Bacc("TRN2", target_bir_lowering=False, num_devices=1)
    arrays = {}

    def give(name, a):
        a = np.ascontiguousarray(a)
        arrays[name] = a
        return nc.dram_tensor(name, a.shape, mybir.dt.from_np(a.dtype), kind="ExternalInput").ap()

    src, dst = np.asarray(src), np.asarray(dst)
    args = [
        give("x_in", np.asarray(x)),
        give("src_c", src.reshape(CHUNKS, P).T),
        give("dst_c", dst.reshape(CHUNKS, P).T),
        give("dst_g", dst.reshape(2, GROUPS // 2, 2 * P).transpose(1, 0, 2)),
        give("gcn_w", np.asarray(L0_gnn_W)), give("gcn_b", np.asarray(L0_gnn_b)),
        [give(f"lstm_w{g}", np.asarray(w)[:, DIM:].T) for g, w in enumerate((L0_ffn_W_i, L0_ffn_W_c, L0_ffn_W_o))],
        [give(f"lstm_b{g}", np.asarray(b)) for g, b in enumerate((L0_ffn_b_i, L0_ffn_b_c, L0_ffn_b_o))],
        [give(f"sage_wn{i}", np.asarray(w)) for i, w in enumerate((L1_gnn_W_neigh0, L1_gnn_W_neigh1))],
        [give(f"sage_ws{i}", np.asarray(w)) for i, w in enumerate((L1_gnn_W_self0, L1_gnn_W_self1))],
        [give(f"sage_b{i}", np.asarray(b)) for i, b in enumerate((L1_gnn_b0, L1_gnn_b1))],
        give("gate_w", np.asarray(L1_ffn_gate_w)), give("gate_b", np.asarray(L1_ffn_gate_b)),
        give("expert_w", np.asarray(L1_ffn_expert_w)), give("expert_b", np.asarray(L1_ffn_expert_b)),
    ]
    out = nc.dram_tensor("out_rows", (NODES, DIM), F32, kind="ExternalOutput").ap()
    build(nc, *args, out)
    r = run_bass_kernel_spmd(nc, [arrays], core_ids=[0])
    return r.results[0]["out_rows"]
```

```python
from contextlib import ExitStack

import concourse.bass as bass
from concourse import mybir

F32 = mybir.dt.float32
F32R = mybir.dt.float32r
BF16 = mybir.dt.bfloat16
U16 = mybir.dt.uint16
I32 = mybir.dt.int32
ALU = mybir.AluOpType
ACT = mybir.ActivationFunctionType
AX = mybir.AxisListType

NODES, DIM, EDGES, EXPERTS = 1250, 1024, 40000, 8
P = 125
TILES = NODES // P
KC = DIM // 128
HALF = DIM // 2
HALVES = 2
CHUNKS = EDGES // P
GROUPS = CHUNKS // 2
WIN = 25
WCOLS = WIN * TILES
MAX_ROUNDS = NODES // WIN
PER_TILE = GROUPS // TILES
SLOTS = 4
LN_EPS = 1e-5
SAGE_LAYERS = 2
THRESHOLD = 0.1
EXACT = 4096

RING = 5
FUSED = 3 * TILES
J_GCN = 0
J_LSTM = J_GCN + HALVES * TILES
J_SAGE = [J_LSTM + FUSED + 5 * TILES + 80 * i for i in range(2)]
J_PREP4 = J_SAGE[1] + 80
J_EXPERT_B = J_PREP4 + 2 * TILES
J_EXPERT = J_EXPERT_B + 2 * TILES
J_END = J_EXPERT + EXPERTS * 2 * TILES
N_LSTM, N_SAGE, N_MOE = 2, [8, 12], 16


def transposed(t, g):
    return g if t == 0 else 3 * t - 1 + g


def first_pass(t):
    return 3 * t + 4 if t < TILES - 1 else FUSED - 1


def build(nc, x, src_c, dst_c, dst_g, gcn_w, gcn_b, lstm_w, lstm_b, sage_wn, sage_ws, sage_b,
          gate_w, gate_b, expert_w, expert_b, out):
    ctx = ExitStack()
    with ctx:
        def dram(name, shape, dt=F32):
            return nc.dram_tensor(name, shape, dt, kind="Internal").ap()

        x1_d, x2_d, h1_d, x3_d = (dram(n, [NODES, DIM]) for n in ("x1_d", "x2_d", "h1_d", "x3_d"))
        counts_d = dram("counts_d", [P, NODES * TILES], U16)
        alo_d = dram("alo_d", [TILES, 2, P, TILES * P // 2])
        stat_d = dram("stat_d", [2, GROUPS])

        def rows(ap):
            return ap.rearrange("(t p) d -> t p d", p=P)

        x_t, x1_t, x2_t, h1_t, x3_t, out_t = map(rows, (x, x1_d, x2_d, h1_d, x3_d, out))

        def sem(name):
            return ctx.enter_context(nc.semaphore(name))

        base = 16512
        used = {}

        def at(name, shape, dt, offset):
            t = nc.alloc_sbuf_tensor_at(name, shape, dt, offset=offset)
            n = 1
            for d in shape[1:]:
                n *= d
            used[name] = offset + n * mybir.dt.size(dt)
            return t

        XT0 = base + 960
        W0 = XT0 + 80960
        Z0 = W0 + 65536
        S0 = Z0 + 40960
        C0 = S0 + 22816
        xt_hi = at("xt_hi", [128, TILES, KC, P], F32R, XT0)
        xt_lo = at("xt_lo", [128, TILES, KC, P], F32R, XT0 + 40000)
        z_raw = at("z_raw", [P, TILES, DIM], F32, XT0 - 960)
        g_hi = at("g_hi", [P, TILES, HALF], F32R, XT0 + 40000)
        g_lo = at("g_lo", [P, TILES, HALF], F32R, XT0 + 60480)
        w_hi = [at(f"w_hi{i}", [128, KC, HALF], F32R, W0 + i * 32768) for i in range(2)]
        w_lo = [at(f"w_lo{i}", [128, KC, HALF], F32R, W0 + i * 32768 + 16384) for i in range(2)]
        w_raw = [at(f"w_raw{i}", [128, KC, HALF], F32, W0 + i * 32768 + 16384) for i in range(2)]
        z_hi = at("z_hi", [P, TILES, HALF], F32R, Z0)
        z_lo = at("z_lo", [P, TILES, HALF], F32R, Z0 + 20480)
        cell = at("cell", [P, TILES, HALF], F32, Z0)
        acc = at("acc", [P, TILES, DIM], F32, Z0)
        counts = at("counts", [P, (NODES + WIN) * TILES], U16, Z0)
        o = Z0 + 25504
        src_p = at("src_p", [P, CHUNKS], F32, o)
        src_b = at("src_b", [P, CHUNKS], F32, o + 1280)
        key = at("key", [P, CHUNKS], F32, o + 2560)
        iota = at("iota", [P, WCOLS], BF16, o + 3840)
        ident_r = at("ident_r", [P, P], F32R, o + 4352)
        hot_p = at("hot_p", [P, SLOTS, 2, P + 1], BF16, o + 4864)
        hot_k = at("hot_k", [P, SLOTS, 2, WCOLS], BF16, o + 6880)
        src_i = at("src_i", [P, CHUNKS], I32, o + 4864)
        dst_i = at("dst_i", [P, CHUNKS], I32, o + 6144)
        gdst = at("gdst", [80, 2, 2 * P], I32, o + 7424)
        base_b = at("base_b", [P, GROUPS], F32, o + 10880)
        base_r = at("base_r", [1, GROUPS], F32, o + 11520)
        span_r = at("span_r", [1, GROUPS], F32, o + 12160)
        addr = at("addr", [1, GROUPS], I32, o + 12800)
        steps_r = at("steps_r", [1, MAX_ROUNDS], F32, o + 13440)
        over_r = at("over_r", [1, MAX_ROUNDS], F32, o + 13664)
        gmin = at("gmin", [80, 2], F32, o + 13888)
        gspan = at("gspan", [80, 2], F32, o + 13920)
        rnd = at("rnd", [1, 4], F32, o + 13952)
        rnd_i = at("rnd_i", [1, 1], I32, o + 13984)
        assert used["rnd_i"] <= S0
        indeg = at("indeg", [P, NODES], F32, o + 4864)
        a_hi = [at(f"a_hi{i}", [P, TILES, P], F32R, S0 + i * 5024) for i in range(2)]
        a_16 = at("a_16", [P, P * TILES], U16, S0 + 10048)
        a_lo = at("a_lo", [P, TILES // 2, P], F32R, S0 + 10048)
        lo_out = at("lo_out", [P, TILES // 2, P], F32, S0 + 10048)
        xo = [at(f"xo{i}", [P, HALF], F32, S0 + 12576 + i * 2048) for i in range(2)]
        tmp = [at(f"tmp{i}", [P, HALF], F32, S0 + 16672 + i * 2048) for i in range(2)]
        lo_hi = at("lo_hi", [P, TILES // 2, P], F32R, S0 + 16672)
        bias = at("bias", [P, HALF], F32, S0 + 20768)
        xin = [at(f"xin{i}", [P, DIM], F32, S0 + i * 4096) for i in range(2)]
        yn = [at(f"yn{i}", [P, DIM], F32, S0 + 8192 + i * 4096) for i in range(2)]
        gw_raw = at("gw_raw", [128, KC, EXPERTS], F32, S0)
        gw_hi = at("gw_hi", [128, KC, EXPERTS], F32R, S0 + 256)
        gw_lo = at("gw_lo", [128, KC, EXPERTS], F32R, S0 + 512)
        gb = at("gb", [P, EXPERTS], F32, S0 + 768)
        lg = at("lg", [P, TILES, EXPERTS], F32, S0 + 800)
        sel = at("sel", [P, TILES, EXPERTS], F32, S0 + 1120)
        r10 = at("r10", [P, TILES], F32, S0 + 1440)
        zero10 = at("zero10", [P, TILES], F32, S0 + 1504)
        wt = at("wt", [EXPERTS, TILES, P], F32, S0 + 1568)
        eb = at("eb", [EXPERTS, DIM], F32, S0 + 16384)
        ident = at("ident", [P, P], F32, C0)
        row_no = at("row_no", [P, 1], F32, C0 + 512)
        ones = at("ones", [P, 1], F32, C0 + 544)
        dinv = at("dinv", [P, TILES], F32, C0 + 576)
        root = at("root", [P, TILES], F32, C0 + 640)
        deg_inv = at("deg_inv", [P, TILES], F32, C0 + 704)
        dmax = at("dmax", [P, 1], F32, C0 + 768)
        dmax_all = at("dmax_all", [P, 1], F32, C0 + 800)
        big_i = at("big_i", [1, 1], I32, C0 + 832)
        bn = [at(f"bn{i}", [P, 2, 6], F32, C0 + 864 + 64 * i) for i in range(2)]
        mv = [at(f"mv{i}", [P, 2], F32, C0 + 992 + 32 * i) for i in range(2)]
        std = [at(f"std{i}", [P, 1], F32, C0 + 1056 + 32 * i) for i in range(2)]
        rstd = [at(f"rstd{i}", [P, 1], F32, C0 + 1120 + 32 * i) for i in range(2)]
        assert used["rstd1"] <= 229368, used["rstd1"]

        ps = [ctx.enter_context(nc.psum_tensor(f"ps{i}", [128, 512], F32)) for i in range(8)]
        t_ps, p_ps, hist_ps, deg_ps = ps[0:2], ps[2:4], ps[5:8], ps[4]

        ps_full = sem("ps_full")
        ps_free = sem("ps_free")
        hi_done = sem("hi_done")
        t_full = sem("t_full")
        t_free = sem("t_free")
        t_hi = sem("t_hi")
        p_full = sem("p_full")
        p_free = sem("p_free")
        dstep = sem("dstep")
        edges_in = sem("edges_in")
        stat_out = sem("stat_out")
        stat_ready = sem("stat_ready")
        stat_in = sem("stat_in")
        iota_done = sem("iota_done")
        const_done = sem("const_done")
        rounds_ready = sem("rounds_ready")
        round_step = sem("round_step")
        round_begun = sem("round_begun")
        hot_ready = sem("hot_ready")
        hist_done = sem("hist_done")
        hist_added = sem("hist_added")
        counts_ready = sem("counts_ready")
        counts_out = sem("counts_out")
        indeg_ready = sem("indeg_ready")
        deg_done = sem("deg_done")
        lo_step = sem("lo_step")
        lo_ready = sem("lo_ready")
        lo_stored = sem("lo_stored")
        dmax_ready = sem("dmax_ready")
        dmax_done = sem("dmax_done")
        big_ready = sem("big_ready")
        dinv_sum = sem("dinv_sum")
        dinv_root = sem("dinv_root")
        dinv_ready = sem("dinv_ready")
        g_hi_done = sem("g_hi_done")
        g_ready = sem("g_ready")
        w_landed = [sem(f"w_landed{i}") for i in range(2)]
        w_turn = sem("w_turn")
        w_hi_made = sem("w_hi_made")
        w_ready = sem("w_ready")
        pass_done = sem("pass_done")
        x_landed = sem("x_landed")
        xin_landed = [sem(f"xin_landed{i}") for i in range(2)]
        acc_landed = [sem(f"acc_landed{i}") for i in range(2)]
        var_ready = sem("var_ready")
        std_ready = sem("std_ready")
        y_ready = sem("y_ready")
        a16_landed = sem("a16_landed")
        a_ready = sem("a_ready")
        alo_landed = sem("alo_landed")
        alo_used = sem("alo_used")
        a_used = sem("a_used")
        res_landed = [sem(f"res_landed{i}") for i in range(2)]
        out_ready = sem("out_ready")
        stored = [sem(f"stored{i}") for i in range(2)]
        bias_landed = sem("bias_landed")
        bias_used = sem("bias_used")
        pre_ready = sem("pre_ready")
        gate_done = sem("gate_done")
        cell_ready = sem("cell_ready")
        tanh_done = sem("tanh_done")
        gate_in = sem("gate_in")
        gw_ready = sem("gw_ready")
        logits_done = sem("logits_done")
        shifted = sem("shifted")
        exp_done = sem("exp_done")
        weights_ready = sem("weights_ready")
        wt_done = sem("wt_done")
        wt_ready = sem("wt_ready")
        final = sem("final")

        def bank(j):
            return ps[j % RING]

        class Steps:

            def __init__(self, eng, s):
                self.eng, self.sem, self.at = eng, s, 0

            def __call__(self, ins):
                ins.then_inc(self.sem, 1)
                self.at = self.at + 1
                self.eng.wait_ge(self.sem, self.at)

        NORMED = {1: 1, 2: 2, 4: 3}
        J_STAGE = {1: J_LSTM, 2: J_SAGE[0], 3: J_SAGE[1], 4: J_PREP4}
        HI0 = {1: 0, 2: 20, 3: 60, 4: 100}
        A0 = {0: 0, 2: 20, 3: 40}
        U0 = {0: 0, 1: 20, 2: 40, 3: 60}

        def job_t(s, t, g):
            return J_STAGE[s] + (2 * t + g if s == 4 else transposed(t, g))

        block = ctx.enter_context(nc.Block())

        @block.sync
        def _(sp):
            sp.dma_start(src_i[:], src_c).then_inc(edges_in, 16)
            sp.dma_start(dst_i[:], dst_c).then_inc(edges_in, 16)
            sp.dma_start(gdst[:], dst_g).then_inc(edges_in, 16)
            sp.wait_ge(stat_ready, 1)
            with nc.allow_non_contiguous_dma(reason="160 numbers"):
                for i, t in enumerate((gmin, gspan)):
                    sp.dma_start(stat_d[i].rearrange("(a g) -> g a", a=2), t[:]).then_inc(stat_out, 16)
            sp.wait_ge(stat_out, 32)
            sp.dma_start(base_b[:], stat_d[0].partition_broadcast(P)).then_inc(stat_in, 16)
            sp.dma_start(base_r[:], stat_d[0:1, :]).then_inc(stat_in, 16)
            sp.dma_start(span_r[:], stat_d[1:2, :]).then_inc(stat_in, 16)
            for t in range(TILES):
                if t:
                    sp.wait_ge(y_ready, t)
                sp.dma_start(xin[0][:], x_t[t]).then_inc(x_landed, 16)

            def load_bias(m, b, h):
                if m:
                    sp.wait_ge(bias_used, m)
                sp.dma_start(bias[:], b[h * HALF:(h + 1) * HALF].partition_broadcast(P)).then_inc(bias_landed, 16)

            def load_res(u, source, t, h):
                if u >= 2:
                    sp.wait_ge(stored[t % 2], 16 * (u // 2))
                sp.dma_start(xo[t % 2][:], source[t][:, h * HALF:(h + 1) * HALF]).then_inc(res_landed[t % 2], 16)

            def store(u, target, t, h):
                sp.wait_ge(out_ready, u + 1)
                sp.dma_start(target[t][:, h * HALF:(h + 1) * HALF], xo[t % 2][:]).then_inc(stored[t % 2], 16)

            def load_a_lo(a, t):
                with sp.If(big > 0):
                    for part in range(2):
                        if a or part:
                            sp.wait_ge(alo_used, 2 * a + part)
                        sp.wait_ge(a_ready, a + 1)
                        sp.dma_start(a_lo[:].rearrange("p b d -> p (b d)").bitcast(F32), alo_d[t, part]).then_inc(alo_landed, 16)

            def load_a_16(a, t):
                sp.wait_ge(a_ready, a)
                with sp.If(big > 0):
                    sp.wait_ge(alo_used, 2 * a)
                sp.dma_start(a_16[:], counts_d[:, t * P * TILES:(t + 1) * P * TILES]).then_inc(a16_landed, 16)

            def prep_loads(s, source):
                for t in range(TILES):
                    if t >= 2:
                        if s in NORMED:
                            sp.wait_ge(y_ready, NORMED[s] * TILES + t - 1)
                        else:
                            sp.wait_ge(ps_full, job_t(s, t - 2, 1) + 1)
                    sp.wait_ge(stored[t % 2], 16 * ((U0[s - 1] + TILES + t) // 2 + 1))
                    sp.dma_start(xin[t % 2][:], source[t]).then_inc(xin_landed[t % 2], 16)

            sp.wait_ge(counts_ready, 1)
            sp.dma_start(counts_d, counts[:, 0:NODES * TILES]).then_inc(counts_out, 16)
            sp.wait_ge(big_ready, 1)
            big = sp.value_load(big_i[:], min_val=0, max_val=1)
            with sp.If(big > 0):
                for n in range(2 * TILES):
                    sp.wait_ge(lo_ready, n + 1)
                    sp.dma_start(alo_d[n // 2, n % 2], lo_out[:].rearrange("p b d -> p (b d)")).then_inc(lo_stored, 16)
                sp.wait_ge(lo_stored, 16 * 2 * TILES)
            sp.wait_ge(t_full, 2 * TILES)
            for h in range(HALVES):
                load_bias(h, gcn_b, h)
                for t in range(TILES):
                    u = h * TILES + t
                    load_res(u, x_t, t, h)
                    load_a_lo(u, t)
                    if t:
                        store(u - 1, x1_t, t - 1, h)
                store(u, x1_t, TILES - 1, h)
            sp.wait_ge(ps_full, J_LSTM)
            load_bias(2, lstm_b[0], 0)
            prep_loads(1, x1_t)
            sp.wait_ge(ps_full, job_t(1, TILES - 1, 1) + 1)
            for h in range(HALVES):
                for g in range(3):
                    if h or g:
                        load_bias(2 + 3 * h + g, lstm_b[g], h)
                for t in range(TILES):
                    u = U0[1] + h * TILES + t
                    load_res(u, x1_t, t, h)
                    if t:
                        store(u - 1, x2_t, t - 1, h)
                store(u, x2_t, TILES - 1, h)
            for layer in range(SAGE_LAYERS):
                s = 2 + layer
                sp.wait_ge(ps_full, J_STAGE[s])
                prep_loads(s, (x2_t, h1_t)[layer])
                sp.wait_ge(ps_full, job_t(s, TILES - 1, 1) + 1)
                if layer == 0:
                    sp.wait_ge(counts_out, 16)
                for h in range(HALVES):
                    load_bias(8 + 2 * layer + h, sage_b[layer], h)
                    for t in range(TILES):
                        u = U0[s] + h * TILES + t
                        a = A0[s] + h * TILES + t
                        load_a_16(a, t)
                        if layer == 1:
                            load_res(u, x2_t, t, h)
                        load_a_lo(a, t)
                        if t:
                            store(u - 1, (h1_t, x3_t)[layer], t - 1, h)
                    store(u, (h1_t, x3_t)[layer], TILES - 1, h)
            sp.wait_ge(ps_free, J_PREP4)
            for i in range(2):
                sp.wait_ge(stored[i], 16 * 4 * TILES)
            sp.dma_start(gw_raw[:], gate_w.rearrange("(k p) e -> p k e", p=128)).then_inc(gate_in, 16)
            sp.dma_start(gb[:], gate_b.partition_broadcast(P)).then_inc(gate_in, 16)
            sp.dma_start(eb[:], expert_b).then_inc(gate_in, 16)
            for t in range(TILES):
                if t >= 2:
                    sp.wait_ge(var_ready, NORMED[4] * TILES + t - 1)
                sp.dma_start(acc[:, t, :], x3_t[t]).then_inc(acc_landed[t % 2], 16)
            for t in range(TILES):
                sp.wait_ge(ps_free, J_END - TILES + t + 1)
                sp.dma_start(out_t[t], acc[:, t, :]).then_inc(final, 16)
            sp.wait_ge(final, 16 * TILES)

        @block.gpsimd
        def _(pool):
            nc.gpsimd.iota(iota[:], [[1, WCOLS]], base=0, channel_multiplier=0,
                           allow_small_or_imprecise_dtypes=True).then_inc(iota_done, 1)
            nc.gpsimd.iota(row_no[:], [[0, 1]], base=0, channel_multiplier=1,
                           allow_small_or_imprecise_dtypes=True).then_inc(iota_done, 1)
            nc.gpsimd.iota(steps_r[:], [[WIN, MAX_ROUNDS]], base=WIN, channel_multiplier=0,
                           allow_small_or_imprecise_dtypes=True).then_inc(iota_done, 1)

            def weights(n, i, source, landed):
                if not (isinstance(n, int) and n < 2):
                    pool.wait_ge(pass_done, n - 1)
                    pool.sem_inc(w_turn, 1)
                pool.dma_start(w_raw[i][:], source).then_inc(w_landed[i], 16)
                pool.wait_ge(w_landed[i], landed)
                pool.sem_inc(w_turn, 1)
                nc.gpsimd.tensor_copy(w_hi[i][:], w_raw[i][:]).then_inc(w_hi_made, 1)
                pool.wait_ge(w_hi_made, n + 1)
                nc.gpsimd.tensor_tensor(out=w_lo[i][:], in0=w_raw[i][:], in1=w_hi[i][:].bitcast(F32),
                                        op=ALU.subtract).then_inc(w_ready, 1)

            def half(w, h):
                return w[:, bass.ds(h * HALF, HALF)].rearrange("(k p) n -> p k n", p=128)

            for n in range(HALVES):
                weights(n, n, half(gcn_w, n), 16)
            pool.wait_ge(dmax_ready, 1)
            nc.gpsimd.partition_all_reduce(dmax_all[:], dmax[:], P, bass.bass_isa.ReduceOp.max).then_inc(dmax_done, 1)
            for n in range(N_LSTM, N_SAGE[0]):
                h, g = divmod(n - N_LSTM, 3)
                weights(n, n % 2, half(lstm_w[g], h), 16 * (n // 2 + 1))
            for layer in range(SAGE_LAYERS):
                with pool.Fori(0, HALVES) as h:
                    for i, w in enumerate((sage_wn[layer], sage_ws[layer])):
                        weights(N_SAGE[layer] + 2 * h + i, i, half(w, h), 16 * (N_SAGE[layer] // 2 + 1) + 16 * h)
            with pool.Fori(0, EXPERTS) as e:
                for h in range(HALVES):
                    source = expert_w[bass.ds(e, 1), :, h * HALF:(h + 1) * HALF].rearrange(
                        "e (k p) n -> p (e k) n", p=128)
                    weights(N_MOE + 2 * e + h, h, source, 16 * (N_MOE // 2 + 1) + 16 * e)

        @block.scalar
        def _(act):
            def z_rows(t):
                for h in range(HALVES):
                    act.wait_ge(p_full, 2 * t + h + 1)
                    if h == 0:
                        act.wait_ge(p_full, 2 * t + 2)
                    act.activation(z_raw[:, bass.ds(t, 1), h * HALF:(h + 1) * HALF],
                                   p_ps[h][0:P, :].unsqueeze(1), ACT.Copy).then_inc(p_free, 1)

            def first_tile(t, rows_too):
                act.wait_ge(var_ready, t + 1)
                act.activation(std[0][:], mv[0][:, 1:2], ACT.Sqrt).then_inc(std_ready, 1)
                for g in range(2):
                    act.wait_ge(t_full, 2 * t + g + 1)
                    act.activation(xt_hi[:, bass.ds(t, 1), 4 * g:4 * g + 4, :].rearrange("p t k n -> p (t k n)"),
                                   t_ps[g][:, 0:4 * P], ACT.Copy).then_inc(t_hi, 1)
                if rows_too:
                    z_rows(t - 1)
            first_tile(0, False)
            with act.Fori(1, TILES) as t:
                first_tile(t, True)
            z_rows(TILES - 1)
            act.wait_ge(dinv_sum, 1)
            act.activation(root[:], dinv[:], ACT.Sqrt).then_inc(dinv_root, 1)

            def expand(a, t, source, landed):
                if a >= 2:
                    act.wait_ge(a_used, a - 1)
                if landed:
                    act.wait_ge(a16_landed, landed)
                act.activation(a_hi[t % 2][:], source.rearrange("p (d b) -> p b d", b=TILES), ACT.Copy).then_inc(a_ready, 1)

            act.wait_ge(counts_ready, 1)
            for h in range(HALVES):
                if h == 0:
                    act.wait_ge(dinv_ready, 1)
                else:
                    act.wait_ge(ps_full, J_GCN + TILES)
                for t in range(TILES):
                    act.activation(g_hi[:, t, :], z_raw[:, t, h * HALF:(h + 1) * HALF], ACT.Copy,
                                   scale=dinv[:, t:t + 1]).then_inc(g_hi_done, 1)
                for t in range(TILES):
                    expand(h * TILES + t, t, counts[:, t * P * TILES:(t + 1) * P * TILES], None)

            def deviation(s, t):
                act.wait_ge(var_ready, NORMED[s] * TILES + t + 1)
                act.activation(std[t % 2][:], mv[t % 2][:, 1:2], ACT.Sqrt).then_inc(std_ready, 1)

            def highs(s, t):
                for g in range(2):
                    j = job_t(s, t, g)
                    act.wait_ge(ps_full, j + 1)
                    act.activation(xt_hi[:, t, 4 * g:4 * g + 4, :].rearrange("p k n -> p (k n)"),
                                   bank(j)[:, 0:4 * P], ACT.Copy).then_inc(hi_done, 1)

            def z_high(j, t):
                act.wait_ge(ps_full, j + 1)
                act.activation(z_hi[:, t, :], bank(j)[0:P, :], ACT.Copy).then_inc(hi_done, 1)

            def gate(n, g, t):
                act.wait_ge(pre_ready, n + 1)
                if g == 0:
                    act.activation(cell[:, t, :], tmp[t % 2][:], ACT.Sigmoid).then_inc(gate_done, 1)
                else:
                    act.activation(tmp[t % 2][:], tmp[t % 2][:], ACT.Tanh if g == 1 else ACT.Sigmoid).then_inc(gate_done, 1)

            def fused(s, first):
                act.wait_ge(ps_full, J_STAGE[s])
                if s in NORMED:
                    deviation(s, 0)
                for t in range(TILES + 1):
                    if s in NORMED and t + 1 < TILES:
                        deviation(s, t + 1)
                    if t < TILES:
                        highs(s, t)
                    if t:
                        first(t - 1)

            act.wait_ge(counts_out, 16)
            fused(1, lambda t: gate(t, 0, t))
            for h in range(HALVES):
                for g in range(3):
                    if h == 0 and g == 0:
                        continue
                    for t in range(TILES):
                        gate(30 * h + 10 * g + t, g, t)
                        if g == 1:
                            act.wait_ge(cell_ready, 10 * h + t + 1)
                            act.activation(cell[:, t, :], cell[:, t, :], ACT.Tanh).then_inc(tanh_done, 1)
                act.wait_ge(out_ready, U0[1] + TILES * (h + 1))
            for layer in range(SAGE_LAYERS):
                s = 2 + layer
                fused(s, lambda t: z_high(J_STAGE[s] + first_pass(t), t))
                for h in range(HALVES):
                    if h:
                        for t in range(TILES):
                            z_high(J_STAGE[s] + FUSED + 2 * TILES + t, t)
                    for t in range(TILES):
                        a = A0[s] + h * TILES + t
                        expand(a, t, a_16[:], 16 * (a - A0[2] + 1))
            act.wait_ge(ps_free, J_PREP4)
            for t in range(TILES):
                deviation(4, t)
                if t:
                    highs(4, t - 1)
            highs(4, TILES - 1)
            act.wait_ge(shifted, 1)
            act.activation(lg[:], lg[:], ACT.Exp).then_inc(exp_done, 1)
            for b in range(3):
                act.wait_ge(wt_done, b + 1)
                n = min(4, TILES - 4 * b)
                act.activation(wt[:, 4 * b:4 * b + n, :].rearrange("e t p -> e (t p)"),
                               ps[RING + b][0:EXPERTS, 0:n * P], ACT.Copy).then_inc(wt_ready, 1)

        @block.vector
        def _(dve):
            step = Steps(dve, dstep)
            V = nc.vector
            dve.wait_ge(edges_in, 48)
            V.tensor_reduce(gmin[:], gdst[:], AX.X, ALU.min)
            step(V.tensor_reduce(gspan[:], gdst[:], AX.X, ALU.max))
            step(V.tensor_tensor(gspan[:], gspan[:], gmin[:], ALU.subtract))
            dve.sem_inc(stat_ready, 1)
            V.memset(counts[:].bitcast(I32), 0)
            dve.wait_ge(iota_done, 3)
            V.tensor_scalar(ident[:], iota[:, 0:P], row_no[:], None, ALU.is_equal).then_inc(const_done, 1)
            V.tensor_scalar(ident_r[:], iota[:, 0:P], row_no[:], None, ALU.is_equal).then_inc(const_done, 1)
            V.memset(ones[:], 1.0).then_inc(const_done, 1)
            step(V.tensor_copy(src_p[:], src_i[:]))
            step(V.tensor_scalar(src_b[:], src_p[:], float(P), None, ALU.is_ge))
            for b in range(2, TILES):
                step(V.scalar_tensor_tensor(src_b[:], src_p[:], float(P * b), src_b[:], ALU.is_ge, ALU.add))
            V.scalar_tensor_tensor(src_p[:], src_b[:], float(-P), src_p[:], ALU.mult, ALU.add)
            step(V.tensor_copy(key[:], dst_i[:]))
            step(V.scalar_tensor_tensor(key[:], key[:], float(TILES), src_b[:], ALU.mult, ALU.add))
            dve.wait_ge(stat_in, 48)
            step(V.scalar_tensor_tensor(
                key[:].rearrange("p (g c) -> p g c", c=2), base_b[:].unsqueeze(2).to_broadcast([P, GROUPS, 2]),
                float(-TILES), key[:].rearrange("p (g c) -> p g c", c=2), ALU.mult, ALU.add))
            step(V.reduce_max(rnd[:, 0:1], span_r[:], AX.X))
            step(V.tensor_scalar(over_r[:], steps_r[:], rnd[:, 0:1], 1.0, ALU.is_le, ALU.add, accum_out=rnd[:, 1:2]))
            step(V.tensor_copy(rnd_i[:], rnd[:, 1:2]))
            for _ in range(3):
                dve.sem_inc(hist_added, 1)
            dve.sem_inc(rounds_ready, 1)

            def window_starts():
                return V.tensor_scalar(addr[:], base_r[:], float(NODES), float(TILES), ALU.min, ALU.mult)

            def load_starts(first, n):
                _, values = nc.values_load_multi_w_load_instructions(
                    addr[0:1, bass.ds(first, n)], engines=[mybir.EngineType.DVE], min_val=0, max_val=NODES * TILES,
                    skip_runtime_bounds_check_because="VectorE clamps the offsets where it makes them")
                return values

            def hots(slot, col0):
                for c in range(2):
                    col = bass.ds(col0 + c, 1)
                    V.tensor_scalar(hot_p[:, slot, c, 0:P], iota[:, 0:P], src_p[:, col], None, ALU.is_equal)
                    last = V.tensor_scalar(hot_k[:, slot, c, :], iota[:], key[:, col], None, ALU.is_equal)
                last.then_inc(hot_ready, 1)

            def add(n, b, start):
                dve.wait_ge(hist_done, n + 1)
                dve.wait_ge(hist_added, n + 3)
                win = counts[:, bass.ds(start, WCOLS)]
                V.tensor_tensor(out=win, in0=hist_ps[b][0:P, 0:WCOLS], in1=win, op=ALU.add).then_inc(hist_added, 1)

            def beside(t, q):
                if q == 1:
                    dve.wait_ge(x_landed, 16 * t + 16)
                    V.bn_stats(bn[0][:, 0, :], xin[0][:, 0:HALF])
                    step(V.bn_stats(bn[0][:, 1, :], xin[0][:, HALF:DIM]))
                    step(V.bn_aggr(mv[0][:], bn[0][:].rearrange("p a b -> p (a b)")))
                    V.tensor_scalar(mv[0][:, 1:2], mv[0][:, 1:2], LN_EPS, None, ALU.add).then_inc(var_ready, 1)
                if q == 3:
                    dve.wait_ge(std_ready, t + 1)
                    step(V.reciprocal(rstd[0][:], std[0][:]))
                    V.tensor_scalar(yn[0][:], xin[0][:], mv[0][:, 0:1], rstd[0][:], ALU.subtract, ALU.mult).then_inc(y_ready, 1)
                if q in (PER_TILE - 3, PER_TILE - 2):
                    g = q - (PER_TILE - 3)
                    dve.wait_ge(t_hi, 2 * t + g + 1)
                    V.tensor_tensor(out=xt_lo[:, t, 4 * g:4 * g + 4, :].rearrange("p k n -> p (k n)"), in0=t_ps[g][:, 0:4 * P],
                                    in1=xt_hi[:, t, 4 * g:4 * g + 4, :].rearrange("p k n -> p (k n)").bitcast(F32),
                                    op=ALU.subtract).then_inc(t_free, 1)

            step(window_starts())
            starts = []
            for n in range(GROUPS + 2):
                if n < GROUPS:
                    hots(n % SLOTS, 2 * n)
                    if n % 4 == 0:
                        starts += load_starts(n, 4)
                    beside(*divmod(n, PER_TILE))
                if n >= 2:
                    add(n - 2, (n - 2) % 3, starts[n - 2])
            rounds = dve.value_load(rnd_i[:], min_val=1, max_val=MAX_ROUNDS)
            with dve.If(rounds > 1):
                rstep = Steps(dve, round_step)
                with dve.Fori(1, rounds) as r:
                    rstep.at = (r - 1) * 3
                    rstep(V.tensor_scalar(key[:], key[:], float(-WCOLS), None, ALU.add))
                    rstep(V.tensor_scalar(base_r[:], base_r[:], float(WIN), None, ALU.add))
                    rstep(window_starts())
                    dve.sem_inc(round_begun, 1)
                    with dve.Fori(0, GROUPS) as g:
                        hots(0, 2 * g)
                        add(r * GROUPS + g, 0, load_starts(g, 1)[0])
            dve.wait_ge(hist_added, rounds * GROUPS + 3)
            dve.sem_inc(counts_ready, 1)
            V.tensor_reduce(indeg[:], counts[:, 0:NODES * TILES].rearrange("p (d b) -> p d b", b=TILES), AX.X, ALU.add)\
                .then_inc(indeg_ready, 1)
            dve.wait_ge(deg_done, 1)
            V.tensor_scalar(dinv[:], deg_ps[0:P, 0:TILES], 1.0, None, ALU.add).then_inc(dinv_sum, 1)
            V.tensor_reduce(dmax[:], deg_ps[0:P, 0:TILES], AX.X, ALU.max).then_inc(dmax_ready, 1)
            step(V.tensor_scalar(deg_inv[:], deg_ps[0:P, 0:TILES], 1.0, None, ALU.max))
            V.reciprocal(deg_inv[:], deg_inv[:])
            dve.wait_ge(dinv_root, 1)
            V.reciprocal(dinv[:], root[:]).then_inc(dinv_ready, 1)
            dve.wait_ge(dinv_ready, 1)
            dve.wait_ge(dmax_done, 1)
            step(V.tensor_scalar(big_i[:], dmax_all[0:1, :], float(EXACT), None, ALU.is_gt))
            dve.sem_inc(big_ready, 1)
            big = dve.value_load(big_i[:], min_val=0, max_val=1)
            with dve.If(big > 0):
                for n in range(2 * TILES):
                    t, part = divmod(n, 2)
                    source = counts[:, t * P * TILES:(t + 1) * P * TILES].rearrange("p (d b) -> p b d", b=TILES)
                    source = source[:, part * (TILES // 2):(part + 1) * (TILES // 2), :]
                    if n:
                        dve.wait_ge(lo_stored, 16 * n)
                    V.tensor_copy(lo_hi[:], source).then_inc(lo_step, 1)
                    dve.wait_ge(lo_step, n + 1)
                    V.tensor_tensor(out=lo_out[:], in0=source, in1=lo_hi[:].bitcast(F32), op=ALU.subtract).then_inc(lo_ready, 1)

            for h in range(HALVES):
                for t in range(TILES):
                    dve.wait_ge(g_hi_done, h * TILES + t + 1)
                    V.scalar_tensor_tensor(g_lo[:, t, :], z_raw[:, t, h * HALF:(h + 1) * HALF], dinv[:, t:t + 1],
                                           g_hi[:, t, :].bitcast(F32), ALU.mult, ALU.subtract).then_inc(g_ready, 1)
                dve.wait_ge(bias_landed, 16 * (h + 1))
                for t in range(TILES):
                    u = h * TILES + t
                    j = J_GCN + u
                    dve.wait_ge(ps_full, j + 1)
                    V.scalar_tensor_tensor(tmp[t % 2][:], bank(j)[0:P, :], dinv[:, t:t + 1],
                                           bias[:], ALU.mult, ALU.add).then_inc(ps_free, 1)
                    dve.wait_ge(ps_free, j + 1)
                    dve.wait_ge(res_landed[t % 2], 16 * (u // 2 + 1))
                    V.scalar_tensor_tensor(xo[t % 2][:], tmp[t % 2][:], 0.0, xo[t % 2][:], ALU.max, ALU.add).then_inc(out_ready, 1)
                dve.sem_inc(bias_used, 1)

            def stats(s, t):
                i = t % 2
                tile = acc[:, t, :] if s == 4 else xin[i][:]
                if s == 4:
                    dve.wait_ge(acc_landed[i], 16 * (t // 2 + 1))
                else:
                    dve.wait_ge(xin_landed[i], 16 * ((s - 1) * TILES // 2 + t // 2 + 1))
                V.bn_stats(bn[i][:, 0, :], tile[:, 0:HALF])
                step(V.bn_stats(bn[i][:, 1, :], tile[:, HALF:DIM]))
                step(V.bn_aggr(mv[i][:], bn[i][:].rearrange("p a b -> p (a b)")))
                V.tensor_scalar(mv[i][:, 1:2], mv[i][:, 1:2], LN_EPS, None, ALU.add).then_inc(var_ready, 1)

            def norm(s, t):
                i = t % 2
                tile = acc[:, t, :] if s == 4 else xin[i][:]
                dve.wait_ge(std_ready, NORMED[s] * TILES + t + 1)
                step(V.reciprocal(rstd[i][:], std[i][:]))
                if t >= 2:
                    dve.wait_ge(ps_full, job_t(s, t - 2, 1) + 1)
                V.tensor_scalar(yn[i][:], tile, mv[i][:, 0:1], rstd[i][:], ALU.subtract, ALU.mult).then_inc(y_ready, 1)

            def lows(s, t):
                for g in range(2):
                    j = job_t(s, t, g)
                    hi = xt_hi[:, t, 4 * g:4 * g + 4, :].rearrange("p k n -> p (k n)")
                    n = 2 * t + g if s in (1, 4) or t == 0 else transposed(t, g)
                    dve.wait_ge(hi_done, HI0[s] + n + 1)
                    V.tensor_tensor(out=xt_lo[:, t, 4 * g:4 * g + 4, :].rearrange("p k n -> p (k n)"),
                                    in0=bank(j)[:, 0:4 * P], in1=hi.bitcast(F32), op=ALU.subtract).then_inc(ps_free, 1)

            def z_low(j, n, t):
                dve.wait_ge(hi_done, n + 1)
                V.tensor_tensor(out=z_lo[:, t, :], in0=bank(j)[0:P, :], in1=z_hi[:, t, :].bitcast(F32),
                                op=ALU.subtract).then_inc(ps_free, 1)

            def fused(s, first):
                for i in range(2):
                    dve.wait_ge(stored[i], 16 * (U0[s - 1] // 2 + TILES))
                if s in NORMED:
                    stats(s, 0)
                    norm(s, 0)
                for t in range(TILES + 1):
                    if s in NORMED and t + 1 < TILES:
                        stats(s, t + 1)
                        norm(s, t + 1)
                    if t < TILES:
                        lows(s, t)
                    if t:
                        first(t - 1)

            def pre_gate(j, n, t):
                dve.wait_ge(ps_full, j + 1)
                if n >= 2:
                    dve.wait_ge(gate_done, n - 1)
                V.tensor_tensor(out=tmp[t % 2][:], in0=bank(j)[0:P, :], in1=bias[:], op=ALU.add).then_inc(ps_free, 1)
                dve.wait_ge(ps_free, j + 1)
                dve.sem_inc(pre_ready, 1)

            def first_gate(t):
                if t == 0:
                    dve.wait_ge(bias_landed, 16 * 3)
                pre_gate(J_LSTM + first_pass(t), t, t)
                if t == TILES - 1:
                    dve.sem_inc(bias_used, 1)
            fused(1, first_gate)
            for h in range(HALVES):
                for g in range(3):
                    if h == 0 and g == 0:
                        continue
                    m = 2 + 3 * h + g
                    dve.wait_ge(bias_landed, 16 * (m + 1))
                    for t in range(TILES):
                        n = 30 * h + 10 * g + t
                        pre_gate(J_LSTM + FUSED + n - TILES, n, t)
                        if g == 1:
                            dve.wait_ge(gate_done, n + 1)
                            V.tensor_tensor(out=cell[:, t, :], in0=cell[:, t, :], in1=tmp[t % 2][:], op=ALU.mult).then_inc(cell_ready, 1)
                        if g == 2:
                            dve.wait_ge(gate_done, n + 1)
                            dve.wait_ge(tanh_done, 10 * h + t + 1)
                            step(V.tensor_tensor(out=tmp[t % 2][:], in0=tmp[t % 2][:], in1=cell[:, t, :], op=ALU.mult))
                            u = U0[1] + 10 * h + t
                            dve.wait_ge(res_landed[t % 2], 16 * (u // 2 + 1))
                            V.tensor_tensor(out=xo[t % 2][:], in0=tmp[t % 2][:], in1=xo[t % 2][:], op=ALU.add).then_inc(out_ready, 1)
                    dve.sem_inc(bias_used, 1)
            for layer in range(SAGE_LAYERS):
                s = 2 + layer
                j0 = J_STAGE[s]

                def z_first(t):
                    n = 3 * t + 4 if t < TILES - 1 else FUSED - 1
                    z_low(j0 + first_pass(t), HI0[s] + n, t)
                fused(s, z_first)
                for h in range(HALVES):
                    if h:
                        for t in range(TILES):
                            z_low(j0 + FUSED + 2 * TILES + t, HI0[s] + FUSED + t, t)
                    dve.wait_ge(bias_landed, 16 * (8 + 2 * layer + h + 1))
                    for t in range(TILES):
                        u = U0[s] + h * TILES + t
                        ja = j0 + FUSED + h * 3 * TILES + 2 * t
                        dve.wait_ge(ps_full, ja + 1)
                        V.scalar_tensor_tensor(tmp[t % 2][:], bank(ja)[0:P, :], deg_inv[:, t:t + 1], bias[:], ALU.mult, ALU.add).then_inc(ps_free, 1)
                        dve.wait_ge(ps_free, ja + 1)
                        dve.wait_ge(ps_full, ja + 2)
                        V.tensor_tensor(out=tmp[t % 2][:], in0=bank(ja + 1)[0:P, :], in1=tmp[t % 2][:], op=ALU.add).then_inc(ps_free, 1)
                        dve.wait_ge(ps_free, ja + 2)
                        if layer == 0:
                            dve.wait_ge(stored[t % 2], 16 * (u // 2))
                            V.tensor_scalar(xo[t % 2][:], tmp[t % 2][:], 0.0, None, ALU.max).then_inc(out_ready, 1)
                        else:
                            dve.wait_ge(res_landed[t % 2], 16 * ((u - TILES * 2) // 2 + 1))
                            V.tensor_tensor(out=xo[t % 2][:], in0=tmp[t % 2][:], in1=xo[t % 2][:], op=ALU.add).then_inc(out_ready, 1)
                    dve.sem_inc(bias_used, 1)
            dve.wait_ge(gate_in, 48)
            step(V.tensor_copy(gw_hi[:], gw_raw[:]))
            V.tensor_tensor(out=gw_lo[:], in0=gw_raw[:], in1=gw_hi[:].bitcast(F32), op=ALU.subtract).then_inc(gw_ready, 1)
            for t in range(TILES + 2):
                if t < TILES:
                    stats(4, t)
                if 1 <= t <= TILES:
                    norm(4, t - 1)
                if t >= 2:
                    lows(4, t - 2)
            shape = [P, TILES, EXPERTS]
            dve.wait_ge(logits_done, 1)
            step(V.tensor_tensor(out=lg[:], in0=ps[RING][0:P, 0:TILES * EXPERTS].rearrange("p (t e) -> p t e", e=EXPERTS),
                                 in1=gb[:].unsqueeze(1).to_broadcast(shape), op=ALU.add))
            step(V.reduce_max(r10[:], lg[:], AX.X))
            V.tensor_tensor(out=lg[:], in0=lg[:], in1=r10[:].unsqueeze(2).to_broadcast(shape), op=ALU.subtract).then_inc(shifted, 1)
            dve.wait_ge(exp_done, 1)
            step(V.reduce_sum(r10[:], lg[:], AX.X))
            step(V.reciprocal(r10[:], r10[:]))
            step(V.tensor_tensor(out=lg[:], in0=lg[:], in1=r10[:].unsqueeze(2).to_broadcast(shape), op=ALU.mult))
            step(V.tensor_scalar(sel[:], lg[:], THRESHOLD, None, ALU.is_ge))
            step(V.tensor_tensor(out=lg[:], in0=lg[:], in1=sel[:], op=ALU.mult))
            step(V.reduce_sum(r10[:], lg[:], AX.X))
            step(V.tensor_scalar(zero10[:], r10[:], 0.0, None, ALU.is_equal))
            step(V.tensor_tensor(out=r10[:], in0=r10[:], in1=zero10[:], op=ALU.add))
            step(V.reciprocal(r10[:], r10[:]))
            step(V.tensor_tensor(out=lg[:], in0=lg[:], in1=r10[:].unsqueeze(2).to_broadcast(shape), op=ALU.mult))
            dve.sem_inc(weights_ready, 1)
            for h in range(HALVES):
                for t in range(TILES):
                    j = J_EXPERT_B + h * TILES + t
                    dve.wait_ge(ps_full, j + 1)
                    part = acc[:, t, h * HALF:(h + 1) * HALF]
                    V.tensor_tensor(out=part, in0=bank(j)[0:P, :], in1=part, op=ALU.add).then_inc(ps_free, 1)
            with dve.Fori(0, EXPERTS) as e:
                for h in range(HALVES):
                    for t in range(TILES):
                        n = h * TILES + t
                        j = J_EXPERT + 2 * TILES * e + n
                        dve.wait_ge(ps_full, j + 1)
                        dve.wait_ge(ps_free, j - 2 * TILES + 1)
                        part = acc[:, t, h * HALF:(h + 1) * HALF]
                        V.scalar_tensor_tensor(part, ps[n % RING][0:P, :], lg[:, t, bass.ds(e, 1)], part,
                                               ALU.mult, ALU.add).then_inc(ps_free, 1)

        @block.tensor
        def _(pe):
            mm = nc.tensor.matmul

            def hist_group(n, slot, b, added):
                pe.wait_ge(hot_ready, n + 1)
                pe.wait_ge(hist_added, added)
                for c in range(2):
                    last = mm(hist_ps[b][0:P, 0:WCOLS], hot_p[:, slot, c, 0:P], hot_k[:, slot, c, :],
                              start=c == 0, stop=c == 1)
                last.then_inc(hist_done, 1)

            PARTS = ((xt_hi, 0), (xt_hi, 1), (xt_lo, 0))

            def products(dst, t, arena, k):
                w = (w_hi[arena], w_lo[arena])
                for n, (xt, i) in enumerate(PARTS):
                    last = mm(dst[0:P, :], xt[:, t, k, :], w[i][:, k, :], start=k == 0 and n == 0, stop=k == KC - 1 and n == 2)
                return last

            def product(dst, t, arena):
                for k in range(KC):
                    last = products(dst, t, arena, k)
                return last

            def transposes(dst, y, g):
                for k in range(4):
                    c = 4 * g + k
                    last = nc.tensor.transpose(dst[:, k * P:(k + 1) * P], y[:, c * 128:(c + 1) * 128], ident[:])
                return last

            pe.wait_ge(const_done, 3)
            pe.wait_ge(rounds_ready, 1)
            for t in range(TILES + 1):
                for q in range(PER_TILE):
                    if t < TILES:
                        n = t * PER_TILE + q
                        hist_group(n, n % SLOTS, n % 3, n + 1)
                    if t:
                        h, k = divmod(q, KC)
                        if q == 0:
                            pe.wait_ge(t_free, 2 * t)
                        if k == 0:
                            pe.wait_ge(w_ready, h + 1)
                            if t >= 2:
                                pe.wait_ge(p_free, 2 * (t - 2) + h + 1)
                        last = products(p_ps[h], t - 1, h, k)
                        if k == KC - 1:
                            last.then_inc(p_full, 1)
                    if t < TILES and q == 8:
                        pe.wait_ge(y_ready, t + 1)
                        for g in range(2):
                            if t:
                                pe.wait_ge(t_free, 2 * (t - 1) + g + 1)
                            transposes(t_ps[g], yn[0], g).then_inc(t_full, 1)
            pe.wait_ge(p_full, 2 * TILES)
            nc.tensor.sem_inc(pass_done, 2)
            rounds = pe.value_load(rnd_i[:], min_val=1, max_val=MAX_ROUNDS)
            with pe.If(rounds > 1):
                with pe.Fori(1, rounds) as r:
                    with pe.Fori(0, GROUPS) as g:
                        hist_group(r * GROUPS + g, 0, 0, r * GROUPS + g + 3)
            pe.wait_ge(indeg_ready, 1)
            for t in range(TILES):
                last = mm(deg_ps[0:P, t:t + 1], indeg[:, t * P:(t + 1) * P], ones[:], start=True, stop=True)
            last.then_inc(deg_done, 1)
            pe.wait_ge(big_ready, 1)
            big = pe.value_load(big_i[:], min_val=0, max_val=1)

            def free(j):
                if not (isinstance(j, int) and j < RING):
                    pe.wait_ge(ps_free, j - RING + 1)

            def aggregate(dst, t, a, hi, lo, own):
                pe.wait_ge(a_ready, a + 1)
                for b in range(TILES):
                    mm(dst[0:P, :], a_hi[t % 2][:, b, :], hi[:, b, :], start=b == 0, stop=False)
                    if b < TILES - 1:
                        mm(dst[0:P, :], a_hi[t % 2][:, b, :], lo[:, b, :], start=False, stop=False)
                if own:
                    mm(dst[0:P, :], ident_r[:], hi[:, t, :], start=False, stop=False)
                    mm(dst[0:P, :], ident_r[:], lo[:, t, :], start=False, stop=False)
                with pe.If(big > 0):
                    for part in range(2):
                        pe.wait_ge(alo_landed, 32 * a + 16 * (part + 1))
                        for b in range(TILES // 2):
                            last = mm(dst[0:P, :], a_lo[:, b, :], hi[:, part * (TILES // 2) + b, :], start=False, stop=False)
                        last.then_inc(alo_used, 1)
                mm(dst[0:P, :], a_hi[t % 2][:, TILES - 1, :], lo[:, TILES - 1, :], start=False, stop=True).then_inc(ps_full, 1)

            for h in range(HALVES):
                pe.wait_ge(g_ready, TILES * (h + 1))
                for t in range(TILES):
                    j = J_GCN + h * TILES + t
                    free(j)
                    aggregate(bank(j), t, h * TILES + t, g_hi, g_lo, True)
                    pe.wait_ge(ps_full, j + 1)
                    nc.tensor.sem_inc(a_used, 1)

            def pass_end(j):
                pe.wait_ge(ps_full, j)
                nc.tensor.sem_inc(pass_done, 1)

            def fused(s, arena, n):
                for t in range(TILES + 1):
                    if t < TILES:
                        if s in NORMED:
                            pe.wait_ge(y_ready, NORMED[s] * TILES + t + 1)
                        else:
                            pe.wait_ge(xin_landed[t % 2], 16 * ((s - 1) * TILES // 2 + t // 2 + 1))
                        for g in range(2):
                            j = job_t(s, t, g)
                            free(j)
                            transposes(bank(j), (yn if s in NORMED else xin)[t % 2], g).then_inc(ps_full, 1)
                    if t:
                        if t == 1:
                            pe.wait_ge(w_ready, n + 1)
                        pe.wait_ge(ps_free, job_t(s, t - 1, 1) + 1)
                        j = J_STAGE[s] + first_pass(t - 1)
                        free(j)
                        product(bank(j), t - 1, arena).then_inc(ps_full, 1)
                pass_end(J_STAGE[s] + FUSED)

            fused(1, 0, N_LSTM)
            for n in range(1, 6):
                pe.wait_ge(w_ready, N_LSTM + n + 1)
                for t in range(TILES):
                    j = J_LSTM + FUSED + (n - 1) * TILES + t
                    free(j)
                    product(bank(j), t, n % 2).then_inc(ps_full, 1)
                pass_end(j + 1)
            for layer in range(SAGE_LAYERS):
                s = 2 + layer
                n = N_SAGE[layer]
                fused(s, 0, n)
                for h in range(HALVES):
                    j0 = J_STAGE[s] + FUSED + h * 3 * TILES
                    if h:
                        pe.wait_ge(w_ready, n + 3)
                        for t in range(TILES):
                            free(j0 - TILES + t)
                            product(bank(j0 - TILES + t), t, 0).then_inc(ps_full, 1)
                        pass_end(j0)
                    pe.wait_ge(ps_free, j0)
                    pe.wait_ge(w_ready, n + 2 * h + 2)
                    for t in range(TILES):
                        ja = j0 + 2 * t
                        free(ja)
                        aggregate(bank(ja), t, A0[s] + h * TILES + t, z_hi, z_lo, False)
                        free(ja + 1)
                        product(bank(ja + 1), t, 1).then_inc(ps_full, 1)
                        pe.wait_ge(ps_full, ja + 1)
                        nc.tensor.sem_inc(a_used, 1)
                    pass_end(j0 + 2 * TILES)
            for t in range(TILES):
                pe.wait_ge(y_ready, NORMED[4] * TILES + t + 1)
                for g in range(2):
                    j = job_t(4, t, g)
                    free(j)
                    transposes(bank(j), yn[t % 2], g).then_inc(ps_full, 1)
            pe.wait_ge(ps_free, J_PREP4 + 2 * TILES)
            pe.wait_ge(gw_ready, 1)
            for t in range(TILES):
                for k in range(KC):
                    for n, (xt, i) in enumerate(PARTS):
                        last = mm(ps[RING][0:P, t * EXPERTS:(t + 1) * EXPERTS], xt[:, t, k, :], (gw_hi, gw_lo)[i][:, k, :],
                                  start=k == 0 and n == 0, stop=k == KC - 1 and n == 2)
            last.then_inc(logits_done, 1)
            pe.wait_ge(weights_ready, 1)
            for b in range(3):
                for t in range(4 * b, min(4 * b + 4, TILES)):
                    last = nc.tensor.transpose(ps[RING + b][0:EXPERTS, (t - 4 * b) * P:(t - 4 * b + 1) * P], lg[:, t, :], ident[:])
                last.then_inc(wt_done, 1)
            pe.wait_ge(wt_ready, 3)
            for h in range(HALVES):
                for t in range(TILES):
                    j = J_EXPERT_B + h * TILES + t
                    free(j)
                    mm(bank(j)[0:P, :], wt[:, t, :], eb[:, h * HALF:(h + 1) * HALF], start=True, stop=True).then_inc(ps_full, 1)
            with pe.Fori(0, EXPERTS) as e:
                for h in range(HALVES):
                    pe.wait_ge(w_ready, N_MOE + 2 * e + h + 1)
                    for t in range(TILES):
                        n = h * TILES + t
                        j = J_EXPERT + 2 * TILES * e + n
                        free(j)
                        product(ps[n % RING], t, h).then_inc(ps_full, 1)
                    pe.wait_ge(ps_full, j + 1)
                    nc.tensor.sem_inc(pass_done, 1)


def kernel(x, src, dst, L0_gnn_W, L0_gnn_b, L0_ffn_W_f, L0_ffn_b_f, L0_ffn_W_i, L0_ffn_b_i, L0_ffn_W_o,
           L0_ffn_b_o, L0_ffn_W_c, L0_ffn_b_c, L1_gnn_W_self0, L1_gnn_W_neigh0, L1_gnn_b0, L1_gnn_W_self1,
           L1_gnn_W_neigh1, L1_gnn_b1, L1_ffn_gate_w, L1_ffn_gate_b, L1_ffn_expert_w, L1_ffn_expert_b):
    import numpy as np
    import concourse.bacc as bacc
    from concourse.bass_utils import run_bass_kernel_spmd

    nc = bacc.Bacc("TRN2", target_bir_lowering=False, num_devices=1)
    arrays = {}

    def give(name, a):
        a = np.ascontiguousarray(a)
        arrays[name] = a
        return nc.dram_tensor(name, a.shape, mybir.dt.from_np(a.dtype), kind="ExternalInput").ap()

    src, dst = np.asarray(src), np.asarray(dst)
    args = [
        give("x_in", np.asarray(x)),
        give("src_c", src.reshape(CHUNKS, P).T),
        give("dst_c", dst.reshape(CHUNKS, P).T),
        give("dst_g", dst.reshape(2, GROUPS // 2, 2 * P).transpose(1, 0, 2)),
        give("gcn_w", np.asarray(L0_gnn_W)), give("gcn_b", np.asarray(L0_gnn_b)),
        [give(f"lstm_w{g}", np.asarray(w)[:, DIM:].T) for g, w in enumerate((L0_ffn_W_i, L0_ffn_W_c, L0_ffn_W_o))],
        [give(f"lstm_b{g}", np.asarray(b)) for g, b in enumerate((L0_ffn_b_i, L0_ffn_b_c, L0_ffn_b_o))],
        [give(f"sage_wn{i}", np.asarray(w)) for i, w in enumerate((L1_gnn_W_neigh0, L1_gnn_W_neigh1))],
        [give(f"sage_ws{i}", np.asarray(w)) for i, w in enumerate((L1_gnn_W_self0, L1_gnn_W_self1))],
        [give(f"sage_b{i}", np.asarray(b)) for i, b in enumerate((L1_gnn_b0, L1_gnn_b1))],
        give("gate_w", np.asarray(L1_ffn_gate_w)), give("gate_b", np.asarray(L1_ffn_gate_b)),
        give("expert_w", np.asarray(L1_ffn_expert_w)), give("expert_b", np.asarray(L1_ffn_expert_b)),
    ]
    out = nc.dram_tensor("out_rows", (NODES, DIM), F32, kind="ExternalOutput").ap()
    build(nc, *args, out)
    r = run_bass_kernel_spmd(nc, [arrays], core_ids=[0])
    return r.results[0]["out_rows"]
```

```python
from contextlib import ExitStack

import concourse.bass as bass
from concourse import mybir

F32 = mybir.dt.float32
F32R = mybir.dt.float32r
BF16 = mybir.dt.bfloat16
U16 = mybir.dt.uint16
I32 = mybir.dt.int32
ALU = mybir.AluOpType
ACT = mybir.ActivationFunctionType
AX = mybir.AxisListType

NODES, DIM, EDGES, EXPERTS = 1250, 1024, 40000, 8
P = 125
TILES = NODES // P
KC = DIM // 128
HALF = DIM // 2
HALVES = 2
CHUNKS = EDGES // P
GROUPS = CHUNKS // 2
WIN = 25
WCOLS = WIN * TILES
MAX_ROUNDS = NODES // WIN
PER_TILE = GROUPS // TILES
SLOTS = 4
LN_EPS = 1e-5
SAGE_LAYERS = 2
THRESHOLD = 0.1
EXACT = 4096

RING = 5
FUSED = 3 * TILES
J_GCN = 0
J_LSTM = J_GCN + HALVES * TILES
J_SAGE = [J_LSTM + FUSED + 5 * TILES + 80 * i for i in range(2)]
J_MOE = J_SAGE[1] + 80
J_SECOND = J_MOE + FUSED
J_EXPERT_B = J_SECOND + TILES
J_EXPERT = J_EXPERT_B + 2 * TILES
J_END = J_EXPERT + (EXPERTS - 1) * 2 * TILES
N_LSTM, N_SAGE, N_MOE = 2, [8, 12], 16


def transposed(t, g):
    return g if t == 0 else 3 * t - 1 + g


def first_pass(t):
    return 3 * t + 4 if t < TILES - 1 else FUSED - 1


def by_scalar(n):
    return n - n // 8


def build(nc, x, src_c, dst_c, dst_g, gcn_w, gcn_b, lstm_w, lstm_b, sage_wn, sage_ws, sage_b,
          gate_w, gate_b, expert_w, expert_b, out):
    ctx = ExitStack()
    with ctx:
        def dram(name, shape, dt=F32):
            return nc.dram_tensor(name, shape, dt, kind="Internal").ap()

        x1_d, x2_d, h1_d, x3_d = (dram(n, [NODES, DIM]) for n in ("x1_d", "x2_d", "h1_d", "x3_d"))
        counts_d = dram("counts_d", [P, NODES * TILES], U16)
        alo_d = dram("alo_d", [TILES, 2, P, TILES * P // 2])
        stat_d = dram("stat_d", [2, GROUPS])

        def rows(ap):
            return ap.rearrange("(t p) d -> t p d", p=P)

        x_t, x1_t, x2_t, h1_t, x3_t, out_t = map(rows, (x, x1_d, x2_d, h1_d, x3_d, out))

        def sem(name):
            return ctx.enter_context(nc.semaphore(name))

        base = 16512
        used = {}

        def at(name, shape, dt, offset):
            t = nc.alloc_sbuf_tensor_at(name, shape, dt, offset=offset)
            n = 1
            for d in shape[1:]:
                n *= d
            used[name] = offset + n * mybir.dt.size(dt)
            return t

        XT0 = base + 960
        W0 = XT0 + 80960
        Z0 = W0 + 65536
        S0 = Z0 + 40960
        C0 = S0 + 22816
        xt_hi = at("xt_hi", [128, TILES, KC, P], F32R, XT0)
        xt_lo = at("xt_lo", [128, TILES, KC, P], F32R, XT0 + 40000)
        z_raw = at("z_raw", [P, TILES, DIM], F32, XT0 - 960)
        g_hi = at("g_hi", [P, TILES, HALF], F32R, XT0 + 40000)
        g_lo = at("g_lo", [P, TILES, HALF], F32R, XT0 + 60480)
        g_hi1 = at("g_hi1", [P, TILES, DIM], F32R, XT0 - 960)
        g_lo1 = at("g_lo1", [P, TILES, HALF], F32R, W0 + 32768)
        w_hi = [at(f"w_hi{i}", [128, KC, HALF], F32R, W0 + i * 32768) for i in range(2)]
        w_lo = [at(f"w_lo{i}", [128, KC, HALF], F32R, W0 + i * 32768 + 16384) for i in range(2)]
        w_raw = [at(f"w_raw{i}", [128, KC, HALF], F32, W0 + i * 32768 + 16384) for i in range(2)]
        z_hi = at("z_hi", [P, TILES, HALF], F32R, Z0)
        z_lo = at("z_lo", [P, TILES, HALF], F32R, Z0 + 20480)
        cell = at("cell", [P, TILES, HALF], F32, Z0)
        acc = at("acc", [P, TILES, DIM], F32, Z0)
        counts = at("counts", [P, (NODES + WIN) * TILES], U16, Z0)
        o = Z0 + 25504
        src_p = at("src_p", [P, CHUNKS], F32, o)
        src_b = at("src_b", [P, CHUNKS], F32, o + 1280)
        key = at("key", [P, CHUNKS], F32, o + 2560)
        iota = at("iota", [P, WCOLS], BF16, o + 3840)
        dinv2 = at("dinv2", [P, TILES], F32, o + 4352)
        hot_p = at("hot_p", [P, SLOTS, 2, P + 1], BF16, o + 4864)
        hot_k = at("hot_k", [P, SLOTS, 2, WCOLS], BF16, o + 6880)
        src_i = at("src_i", [P, CHUNKS], I32, o + 4864)
        dst_i = at("dst_i", [P, CHUNKS], I32, o + 6144)
        gdst = at("gdst", [80, 2, 2 * P], I32, o + 7424)
        base_b = at("base_b", [P, GROUPS], F32, o + 10880)
        base_r = at("base_r", [1, GROUPS], F32, o + 11520)
        span_r = at("span_r", [1, GROUPS], F32, o + 12160)
        addr = at("addr", [1, GROUPS], I32, o + 12800)
        steps_r = at("steps_r", [1, MAX_ROUNDS], F32, o + 13440)
        over_r = at("over_r", [1, MAX_ROUNDS], F32, o + 13664)
        gmin = at("gmin", [80, 2], F32, o + 13888)
        gspan = at("gspan", [80, 2], F32, o + 13920)
        rnd = at("rnd", [1, 4], F32, o + 13952)
        rnd_i = at("rnd_i", [1, 1], I32, o + 13984)
        assert used["rnd_i"] <= S0
        indeg = at("indeg", [P, NODES], F32, o + 4864)
        a_hi = [at(f"a_hi{i}", [P, TILES, P], F32R, S0 + i * 5024) for i in range(2)]
        a_16 = at("a_16", [P, P * TILES], U16, S0 + 10048)
        a_lo = at("a_lo", [P, TILES // 2, P], F32R, S0 + 10048)
        lo_out = at("lo_out", [P, TILES // 2, P], F32, S0 + 10048)
        xo = [at(f"xo{i}", [P, HALF], F32, S0 + 12576 + i * 2048) for i in range(2)]
        tmp = [at(f"tmp{i}", [P, HALF], F32, S0 + 16672 + i * 2048) for i in range(2)]
        lo_hi = at("lo_hi", [P, TILES // 2, P], F32R, S0 + 16672)
        bias = at("bias", [P, HALF], F32, S0 + 20768)
        xin = [at(f"xin{i}", [P, DIM], F32, S0 + i * 4096) for i in range(2)]
        dist = at("dist", [P, 3, 2, P], BF16, S0 + 4096)
        x_early = [at(f"x_early{i}", [P, DIM], F32, W0 + 53248 + i * 4096) for i in range(2)]
        yn = [at(f"yn{i}", [P, DIM], F32, S0 + (8192, 16672)[i]) for i in range(2)]
        gw_raw = at("gw_raw", [128, KC, EXPERTS], F32, S0)
        gw = at("gw", [128, KC, 2, EXPERTS], F32R, S0 + 256)
        gb = at("gb", [P, EXPERTS], F32, S0 + 768)
        lg = at("lg", [P, TILES, EXPERTS], F32, S0 + 800)
        sel = at("sel", [P, TILES, EXPERTS], F32, S0 + 1120)
        r10 = at("r10", [P, TILES], F32, S0 + 1440)
        zero10 = at("zero10", [P, TILES], F32, S0 + 1504)
        wt = at("wt", [EXPERTS, TILES, P], F32, S0 + 1568)
        eb = at("eb", [EXPERTS, DIM], F32, S0 + 12576)
        ident = at("ident", [P, P], F32, C0)
        row_no = at("row_no", [P, 1], F32, C0 + 512)
        ones = at("ones", [P, 1], F32, C0 + 544)
        dinv = at("dinv", [P, TILES], F32, C0 + 576)
        root = at("root", [P, TILES], F32, C0 + 640)
        deg_inv = at("deg_inv", [P, TILES], F32, C0 + 704)
        dmax = at("dmax", [P, 1], F32, C0 + 768)
        dmax_all = at("dmax_all", [P, 1], F32, C0 + 800)
        big_i = at("big_i", [1, 1], I32, C0 + 832)
        bn = [at(f"bn{i}", [P, 2, 6], F32, C0 + 864 + 64 * i) for i in range(2)]
        mv = [at(f"mv{i}", [P, 2], F32, C0 + 992 + 32 * i) for i in range(2)]
        std = [at(f"std{i}", [P, 1], F32, C0 + 1056 + 32 * i) for i in range(2)]
        rstd = [at(f"rstd{i}", [P, 1], F32, C0 + 1120 + 32 * i) for i in range(2)]
        assert used["rstd1"] <= 229368, used["rstd1"]

        ps = [ctx.enter_context(nc.psum_tensor(f"ps{i}", [128, 512], F32)) for i in range(8)]
        t_ps, p_ps, hist_ps, deg_ps = ps[0:2], ps[2:5], ps[5:8], ps[7]

        def p_bank(t, h):
            return p_ps[1] if h else p_ps[2 * (t % 2)]

        ps_full = sem("ps_full")
        ps_free = sem("ps_free")
        hi_done = sem("hi_done")
        t_full = sem("t_full")
        t_free = sem("t_free")
        t_hi = sem("t_hi")
        p_full = sem("p_full")
        p_free = sem("p_free")
        dstep = sem("dstep")
        edges_in = sem("edges_in")
        stat_out = sem("stat_out")
        stat_ready = sem("stat_ready")
        stat_in = sem("stat_in")
        iota_done = sem("iota_done")
        const_done = sem("const_done")
        rounds_ready = sem("rounds_ready")
        round_step = sem("round_step")
        round_begun = sem("round_begun")
        zeroed = sem("zeroed")
        dist_done = sem("dist_done")
        hot_p_ready = sem("hot_p_ready")
        hot_ready = sem("hot_ready")
        hist_done = sem("hist_done")
        hist_added = sem("hist_added")
        counts_ready = sem("counts_ready")
        counts_out = sem("counts_out")
        indeg_ready = sem("indeg_ready")
        deg_done = sem("deg_done")
        lo_step = sem("lo_step")
        lo_ready = sem("lo_ready")
        lo_stored = sem("lo_stored")
        dmax_ready = sem("dmax_ready")
        dmax_done = sem("dmax_done")
        big_ready = sem("big_ready")
        dinv_sum = sem("dinv_sum")
        dinv_root = sem("dinv_root")
        dinv_ready = sem("dinv_ready")
        g_hi_done = sem("g_hi_done")
        g_ready = sem("g_ready")
        w_landed = [sem(f"w_landed{i}") for i in range(2)]
        gcn_w_landed = [sem(f"gcn_w_landed{i}") for i in range(2)]
        w_turn = sem("w_turn")
        w_hi_made = sem("w_hi_made")
        part_hi_made = sem("part_hi_made")
        part_ready = sem("part_ready")
        w_ready = sem("w_ready")
        pass_done = sem("pass_done")
        x_landed = sem("x_landed")
        xin_landed = [sem(f"xin_landed{i}") for i in range(2)]
        acc_landed = [sem(f"acc_landed{t}") for t in range(TILES)]
        var_ready = sem("var_ready")
        std_ready = sem("std_ready")
        y_ready = sem("y_ready")
        a16_landed = sem("a16_landed")
        a_ready = sem("a_ready")
        alo_landed = sem("alo_landed")
        alo_used = sem("alo_used")
        res_landed = [sem(f"res_landed{i}") for i in range(2)]
        out_ready = sem("out_ready")
        stored = [sem(f"stored{i}") for i in range(2)]
        bias_landed = sem("bias_landed")
        bias_used = sem("bias_used")
        pre_ready = sem("pre_ready")
        gate_done = sem("gate_done")
        cell_ready = sem("cell_ready")
        tanh_done = sem("tanh_done")
        gate_in = sem("gate_in")
        eb_in = sem("eb_in")
        gw_ready = sem("gw_ready")
        logits_done = sem("logits_done")
        shifted = sem("shifted")
        exp_done = sem("exp_done")
        weights_ready = sem("weights_ready")
        wt_done = sem("wt_done")
        wt_ready = sem("wt_ready")
        final = sem("final")

        def bank(j):
            return ps[j % RING]

        class Steps:

            def __init__(self, eng, s):
                self.eng, self.sem, self.at = eng, s, 0

            def __call__(self, ins):
                ins.then_inc(self.sem, 1)
                self.at = self.at + 1
                self.eng.wait_ge(self.sem, self.at)

        NORMED = {1: 1, 2: 2, 4: 3}
        J_STAGE = {1: J_LSTM, 2: J_SAGE[0], 3: J_SAGE[1], 4: J_MOE}
        HI0 = {1: 0, 2: 20, 3: 60, 4: 100}
        A0 = {0: 0, 2: 20, 3: 40}
        U0 = {0: 0, 1: 20, 2: 40, 3: 60}

        def job_t(s, t, g):
            return J_STAGE[s] + transposed(t, g)

        def x_buf(s, t):
            return x_early[t] if s == 1 and t < 2 else xin[t % 2]

        block = ctx.enter_context(nc.Block())

        @block.sync
        def _(sp):
            sp.dma_start(gdst[:], dst_g).then_inc(edges_in, 16)
            sp.dma_start(src_i[:], src_c).then_inc(edges_in, 16)
            sp.dma_start(dst_i[:], dst_c).then_inc(edges_in, 16)
            sp.wait_ge(stat_ready, 1)
            with nc.allow_non_contiguous_dma(reason="160 numbers"):
                for i, t in enumerate((gmin, gspan)):
                    sp.dma_start(stat_d[i].rearrange("(a g) -> g a", a=2), t[:]).then_inc(stat_out, 16)
            sp.wait_ge(stat_out, 32)
            sp.dma_start(base_b[:], stat_d[0].partition_broadcast(P)).then_inc(stat_in, 16)
            sp.dma_start(base_r[:], stat_d[0:1, :]).then_inc(stat_in, 16)
            sp.dma_start(span_r[:], stat_d[1:2, :]).then_inc(stat_in, 16)
            for t in range(TILES):
                if t:
                    sp.wait_ge(y_ready, t)
                sp.dma_start(xin[0][:], x_t[t]).then_inc(x_landed, 16)
                if t == 0:
                    for h in range(HALVES):
                        sp.dma_start(w_raw[h][:], gcn_w[:, h * HALF:(h + 1) * HALF].rearrange("(k p) n -> p k n", p=128))\
                            .then_inc(gcn_w_landed[h], 16)

            def load_bias(m, b, h):
                if m:
                    sp.wait_ge(bias_used, m)
                sp.dma_start(bias[:], b[h * HALF:(h + 1) * HALF].partition_broadcast(P)).then_inc(bias_landed, 16)

            def load_res(u, source, t, h):
                if u >= 2:
                    sp.wait_ge(stored[t % 2], 16 * (u // 2))
                sp.dma_start(xo[t % 2][:], source[t][:, h * HALF:(h + 1) * HALF]).then_inc(res_landed[t % 2], 16)

            def store(u, target, t, h):
                sp.wait_ge(out_ready, u + 1)
                sp.dma_start(target[t][:, h * HALF:(h + 1) * HALF], xo[t % 2][:]).then_inc(stored[t % 2], 16)

            def load_a_lo(a, t):
                with sp.If(big > 0):
                    for part in range(2):
                        if a or part:
                            sp.wait_ge(alo_used, 2 * a + part)
                        sp.wait_ge(a_ready, a + 1)
                        sp.dma_start(a_lo[:].rearrange("p b d -> p (b d)").bitcast(F32), alo_d[t, part]).then_inc(alo_landed, 16)

            def load_a_16(a, t):
                sp.wait_ge(a_ready, a)
                with sp.If(big > 0):
                    sp.wait_ge(alo_used, 2 * a)
                sp.dma_start(a_16[:], counts_d[:, t * P * TILES:(t + 1) * P * TILES]).then_inc(a16_landed, 16)

            def prep_loads(s, source, first, last):
                for t in range(first, last):
                    if t >= 2:
                        sp.wait_ge(ps_full, job_t(s, t - 2, 1) + 1)
                    sp.wait_ge(stored[t % 2], 16 * ((U0[s - 1] + TILES + t) // 2 + 1))
                    sp.dma_start(x_buf(s, t)[:], source[t]).then_inc(xin_landed[t % 2], 16)

            def acc_load(t):
                sp.wait_ge(stored[t % 2], 16 * ((U0[3] + TILES + t) // 2 + 1))
                sp.dma_start(acc[:, t, :], x3_t[t]).then_inc(acc_landed[t], 16)

            sp.wait_ge(counts_ready, 1)
            sp.dma_start(counts_d, counts[:, 0:NODES * TILES]).then_inc(counts_out, 16)
            sp.wait_ge(big_ready, 1)
            big = sp.value_load(big_i[:], min_val=0, max_val=1)
            with sp.If(big > 0):
                for n in range(2 * TILES):
                    sp.wait_ge(lo_ready, n + 1)
                    sp.dma_start(alo_d[n // 2, n % 2], lo_out[:].rearrange("p b d -> p (b d)")).then_inc(lo_stored, 16)
                sp.wait_ge(lo_stored, 16 * 2 * TILES)
            for h in range(HALVES):
                load_bias(h, gcn_b, h)
                for t in range(TILES):
                    u = h * TILES + t
                    load_res(u, x_t, t, h)
                    load_a_lo(u, t)
                    if t:
                        store(u - 1, x1_t, t - 1, h)
                    if h and t == 4:
                        prep_loads(1, x1_t, 0, 2)
                store(u, x1_t, TILES - 1, h)
            load_bias(2, lstm_b[0], 0)
            prep_loads(1, x1_t, 2, TILES)
            for h in range(HALVES):
                for g in range(3):
                    if h or g:
                        load_bias(2 + 3 * h + g, lstm_b[g], h)
                for t in range(TILES):
                    u = U0[1] + h * TILES + t
                    load_res(u, x1_t, t, h)
                    if t:
                        store(u - 1, x2_t, t - 1, h)
                    if h and t == 4:
                        prep_loads(2, x2_t, 0, 2)
                store(u, x2_t, TILES - 1, h)
            for layer in range(SAGE_LAYERS):
                s = 2 + layer
                prep_loads(s, (x2_t, h1_t)[layer], 2, TILES)
                sp.wait_ge(ps_full, job_t(s, TILES - 1, 1) + 1)
                if layer == 0:
                    sp.wait_ge(counts_out, 16)
                for h in range(HALVES):
                    load_bias(8 + 2 * layer + h, sage_b[layer], h)
                    for t in range(TILES):
                        u = U0[s] + h * TILES + t
                        a = A0[s] + h * TILES + t
                        load_a_16(a, t)
                        if layer == 1:
                            load_res(u, x2_t, t, h)
                        load_a_lo(a, t)
                        if t:
                            store(u - 1, (h1_t, x3_t)[layer], t - 1, h)
                    if h and layer == 0:
                        for i in range(2):
                            sp.wait_ge(ps_full, J_STAGE[3] - 3 + 2 * i)
                            prep_loads(3, h1_t, i, i + 1)
                    if h and layer == 1:
                        sp.wait_ge(ps_full, J_MOE - 1)
                        acc_load(0)
                        sp.dma_start(gw_raw[:], gate_w.rearrange("(k p) e -> p k e", p=128)).then_inc(gate_in, 16)
                        sp.dma_start(gb[:], gate_b.partition_broadcast(P)).then_inc(gate_in, 16)
                        for i in range(1, 6):
                            acc_load(i)
                    store(u, (h1_t, x3_t)[layer], TILES - 1, h)
            for t in range(6, TILES):
                acc_load(t)
            sp.dma_start(eb[:], expert_b).then_inc(eb_in, 16)
            for t in range(TILES):
                sp.wait_ge(ps_free, J_END - TILES + t + 1)
                sp.dma_start(out_t[t], acc[:, t, :]).then_inc(final, 16)
            sp.wait_ge(final, 16 * TILES)

        @block.gpsimd
        def _(pool):
            nc.gpsimd.iota(iota[:], [[1, WCOLS]], base=0, channel_multiplier=0,
                           allow_small_or_imprecise_dtypes=True).then_inc(iota_done, 1)
            nc.gpsimd.iota(row_no[:], [[0, 1]], base=0, channel_multiplier=1,
                           allow_small_or_imprecise_dtypes=True).then_inc(iota_done, 1)
            nc.gpsimd.iota(steps_r[:], [[WIN, MAX_ROUNDS]], base=WIN, channel_multiplier=0,
                           allow_small_or_imprecise_dtypes=True).then_inc(iota_done, 1)

            def split(n, i):
                nc.gpsimd.tensor_copy(w_hi[i][:], w_raw[i][:]).then_inc(w_hi_made, 1)
                pool.wait_ge(w_hi_made, n + 1)
                nc.gpsimd.tensor_tensor(out=w_lo[i][:], in0=w_raw[i][:], in1=w_hi[i][:].bitcast(F32),
                                        op=ALU.subtract).then_inc(w_ready, 1)

            def weights(n, i, source, landed):
                pool.wait_ge(pass_done, n - 1)
                pool.sem_inc(w_turn, 1)
                pool.dma_start(w_raw[i][:], source).then_inc(w_landed[i], 16)
                pool.wait_ge(w_landed[i], landed)
                pool.sem_inc(w_turn, 1)
                split(n, i)

            def half(w, h):
                return w[:, bass.ds(h * HALF, HALF)].rearrange("(k p) n -> p k n", p=128)

            nc.gpsimd.memset(counts[:].bitcast(I32), 0).then_inc(zeroed, 1)
            pool.wait_ge(gcn_w_landed[0], 16)
            split(0, 0)
            pool.wait_ge(gcn_w_landed[1], 16)
            first, rest = slice(0, KC // 2), slice(KC // 2, KC)
            nc.gpsimd.tensor_copy(w_hi[1][:, first], w_raw[1][:, first]).then_inc(part_hi_made, 1)
            pool.wait_ge(part_hi_made, 1)
            nc.gpsimd.tensor_tensor(out=w_lo[1][:, first], in0=w_raw[1][:, first], in1=w_hi[1][:, first].bitcast(F32),
                                    op=ALU.subtract).then_inc(part_ready, 1)
            nc.gpsimd.tensor_copy(w_hi[1][:, rest], w_raw[1][:, rest]).then_inc(w_hi_made, 1)
            pool.wait_ge(w_hi_made, 2)
            nc.gpsimd.tensor_tensor(out=w_lo[1][:, rest], in0=w_raw[1][:, rest], in1=w_hi[1][:, rest].bitcast(F32),
                                    op=ALU.subtract).then_inc(w_ready, 1)
            pool.wait_ge(dmax_ready, 1)
            nc.gpsimd.partition_all_reduce(dmax_all[:], dmax[:], P, bass.bass_isa.ReduceOp.max).then_inc(dmax_done, 1)
            for n in range(N_LSTM, N_SAGE[0]):
                h, g = divmod(n - N_LSTM, 3)
                weights(n, n % 2, half(lstm_w[g], h), 16 * (n // 2))
            for layer in range(SAGE_LAYERS):
                with pool.Fori(0, HALVES) as h:
                    for i, w in enumerate((sage_wn[layer], sage_ws[layer])):
                        weights(N_SAGE[layer] + 2 * h + i, i, half(w, h), 16 * (N_SAGE[layer] // 2) + 16 * h)
            with pool.Fori(0, EXPERTS) as e:
                for h in range(HALVES):
                    source = expert_w[bass.ds(e, 1), :, h * HALF:(h + 1) * HALF].rearrange(
                        "e (k p) n -> p (e k) n", p=128)
                    weights(N_MOE + 2 * e + h, h, source, 16 * (N_MOE // 2) + 16 * e)

        @block.scalar
        def _(act):
            def distances(n, m):
                if m >= 3:
                    act.wait_ge(hot_p_ready, m - 2)
                for c in range(2):
                    last = act.activation(dist[:, m % 3, c, :], iota[:, 0:P], ACT.Abs, scale=-1.0,
                                          bias=src_p[:, 2 * n + c:2 * n + c + 1])
                last.then_inc(dist_done, 1)

            def one_hots(n, m):
                act.wait_ge(dist_done, m + 1)
                if n >= SLOTS:
                    act.wait_ge(hist_done, n - SLOTS + 1)
                act.activation(hot_p[:, n % SLOTS, :, 0:P], dist[:, m % 3], ACT.Relu, scale=-1.0,
                               bias=ones[:]).then_inc(hot_p_ready, 1)

            def z_rows(t):
                for h in range(HALVES):
                    act.wait_ge(p_full, 2 * t + 2)
                    act.activation(z_raw[:, t, h * HALF:(h + 1) * HALF], p_bank(t, h)[0:P, :], ACT.Copy).then_inc(p_free, 1)

            act.wait_ge(const_done, 2)
            act.activation(std[1][:], ones[:], ACT.Sqrt)
            act.wait_ge(rounds_ready, 1)
            distances(0, 0)
            for n in range(GROUPS):
                t, q = divmod(n, PER_TILE)
                if n % 8 < 7:
                    m = by_scalar(n)
                    after = n + 1 if n % 8 < 6 else n + 2
                    if after < GROUPS:
                        distances(after, m + 1)
                    one_hots(n, m)
                if q == 2:
                    act.wait_ge(var_ready, t + 1)
                    act.activation(std[0][:], mv[0][:, 1:2], ACT.Sqrt).then_inc(std_ready, 1)
                if q == 5 and t >= 3:
                    z_rows(t - 3)
                if q in (11, 12):
                    g = q - 11
                    act.wait_ge(t_full, 2 * t + g + 1)
                    act.activation(xt_hi[:, t, 4 * g:4 * g + 4, :].rearrange("p k n -> p (k n)"),
                                   t_ps[g][:, 0:4 * P], ACT.Copy).then_inc(t_hi, 1)
            for t in range(TILES - 3, TILES - 1):
                z_rows(t)
            act.wait_ge(dinv_sum, 1)
            act.activation(root[:], dinv[:], ACT.Sqrt).then_inc(dinv_root, 1)

            def expand(a, t, source, landed, used):
                if used:
                    act.wait_ge(ps_full, used)
                if landed:
                    act.wait_ge(a16_landed, landed)
                act.activation(a_hi[t % 2][:], source.rearrange("p (d b) -> p b d", b=TILES), ACT.Copy).then_inc(a_ready, 1)

            act.wait_ge(counts_ready, 1)
            act.wait_ge(dinv_ready, 1)
            for t in range(TILES):
                if t == TILES - 1:
                    expand(0, 0, counts[:, 0:P * TILES], None, None)
                    z_rows(t)
                    act.wait_ge(p_free, 2 * TILES)
                act.activation(g_hi[:, t, :], z_raw[:, t, 0:HALF], ACT.Copy, scale=dinv[:, t:t + 1]).then_inc(g_hi_done, 1)
            for a in range(1, 2 * TILES):
                t = a % TILES
                expand(a, t, counts[:, t * P * TILES:(t + 1) * P * TILES], None, J_GCN + a - 1 if a >= 2 else None)
                if a <= TILES:
                    act.wait_ge(out_ready, a)
                    act.activation(g_hi1[:, a - 1, 0:HALF], z_raw[:, a - 1, HALF:DIM], ACT.Copy,
                                   scale=dinv[:, a - 1:a]).then_inc(g_hi_done, 1)

            def deviation(s, t):
                act.wait_ge(var_ready, NORMED[s] * TILES + t + 1)
                act.activation(std[t % 2][:], mv[t % 2][:, 1:2], ACT.Sqrt).then_inc(std_ready, 1)

            def highs(s, t):
                for g in range(2):
                    j = job_t(s, t, g)
                    act.wait_ge(ps_full, j + 1)
                    act.activation(xt_hi[:, t, 4 * g:4 * g + 4, :].rearrange("p k n -> p (k n)"),
                                   bank(j)[:, 0:4 * P], ACT.Copy).then_inc(hi_done, 1)

            def z_high(j, t):
                act.wait_ge(ps_full, j + 1)
                act.activation(z_hi[:, t, :], bank(j)[0:P, :], ACT.Copy).then_inc(hi_done, 1)

            def gate(n, g, t):
                act.wait_ge(pre_ready, n + 1)
                if g == 0:
                    act.activation(cell[:, t, :], cell[:, t, :], ACT.Sigmoid).then_inc(gate_done, 1)
                else:
                    act.activation(tmp[t % 2][:], tmp[t % 2][:], ACT.Tanh if g == 1 else ACT.Sigmoid).then_inc(gate_done, 1)

            def fused(s, first):
                for t in range(TILES + 1):
                    if s in NORMED and 2 <= t + 1 < TILES:
                        deviation(s, t + 1)
                    if t < TILES:
                        highs(s, t)
                    if t:
                        first(t - 1)

            deviation(1, 0)
            deviation(1, 1)
            fused(1, lambda t: gate(t, 0, t))
            for h in range(HALVES):
                for g in range(3):
                    if h == 0 and g == 0:
                        continue
                    for t in range(TILES):
                        if h == 1 and g == 2 and t == 6:
                            deviation(2, 0)
                            deviation(2, 1)
                        gate(30 * h + 10 * g + t, g, t)
                        if g == 1:
                            act.wait_ge(cell_ready, 10 * h + t + 1)
                            act.activation(cell[:, t, :], cell[:, t, :], ACT.Tanh).then_inc(tanh_done, 1)
            for layer in range(SAGE_LAYERS):
                s = 2 + layer

                def adjacency(h, t):
                    a = A0[s] + h * TILES + t
                    expand(a, t, a_16[:], 16 * (a - A0[2] + 1),
                           J_STAGE[s] + FUSED + h * 3 * TILES + 2 * t - 3 if t >= 2 else None)

                def z_part(h, j, t):
                    if t == TILES - 1:
                        adjacency(h, 0)
                    z_high(j, t)

                fused(s, lambda t: z_part(0, J_STAGE[s] + first_pass(t), t))
                for h in range(HALVES):
                    if h:
                        for t in range(TILES):
                            z_part(1, J_STAGE[s] + FUSED + 2 * TILES + t, t)
                    for t in range(1, TILES):
                        adjacency(h, t)
            deviation(4, 0)
            deviation(4, 1)
            for t in range(TILES + 1):
                if t < TILES:
                    highs(4, t)
                if t:
                    act.wait_ge(shifted, t)
                    act.activation(lg[:, t - 1, :], lg[:, t - 1, :], ACT.Exp).then_inc(exp_done, 1)
                if t + 2 < TILES:
                    deviation(4, t + 2)
            for b in range(3):
                act.wait_ge(wt_done, b + 1)
                n = min(4, TILES - 4 * b)
                act.activation(wt[:, 4 * b:4 * b + n, :].rearrange("e t p -> e (t p)"),
                               ps[RING + b][0:EXPERTS, 0:n * P], ACT.Copy).then_inc(wt_ready, 1)

        @block.vector
        def _(dve):
            step = Steps(dve, dstep)
            V = nc.vector
            dve.wait_ge(edges_in, 48)
            V.tensor_reduce(gmin[:], gdst[:], AX.X, ALU.min)
            step(V.tensor_reduce(gspan[:], gdst[:], AX.X, ALU.max))
            step(V.tensor_tensor(gspan[:], gspan[:], gmin[:], ALU.subtract))
            dve.sem_inc(stat_ready, 1)
            dve.wait_ge(iota_done, 3)
            V.tensor_scalar(ident[:], iota[:, 0:P], row_no[:], None, ALU.is_equal).then_inc(const_done, 1)
            V.memset(ones[:], 1.0).then_inc(const_done, 1)
            step(V.tensor_copy(src_p[:], src_i[:]))
            step(V.tensor_scalar(src_b[:], src_p[:], float(P), None, ALU.is_ge))
            for b in range(2, TILES):
                step(V.scalar_tensor_tensor(src_b[:], src_p[:], float(P * b), src_b[:], ALU.is_ge, ALU.add))
            V.scalar_tensor_tensor(src_p[:], src_b[:], float(-P), src_p[:], ALU.mult, ALU.add)
            step(V.tensor_copy(key[:], dst_i[:]))
            step(V.scalar_tensor_tensor(key[:], key[:], float(TILES), src_b[:], ALU.mult, ALU.add))
            dve.wait_ge(stat_in, 48)
            step(V.scalar_tensor_tensor(
                key[:].rearrange("p (g c) -> p g c", c=2), base_b[:].unsqueeze(2).to_broadcast([P, GROUPS, 2]),
                float(-TILES), key[:].rearrange("p (g c) -> p g c", c=2), ALU.mult, ALU.add))
            step(V.reduce_max(rnd[:, 0:1], span_r[:], AX.X))
            step(V.tensor_scalar(over_r[:], steps_r[:], rnd[:, 0:1], 1.0, ALU.is_le, ALU.add, accum_out=rnd[:, 1:2]))
            step(V.tensor_copy(rnd_i[:], rnd[:, 1:2]))
            for _ in range(3):
                dve.sem_inc(hist_added, 1)
            dve.sem_inc(rounds_ready, 1)

            def window_starts():
                return V.tensor_scalar(addr[:], base_r[:], float(NODES), float(TILES), ALU.min, ALU.mult)

            def load_starts(first, n):
                _, values = nc.values_load_multi_w_load_instructions(
                    addr[0:1, bass.ds(first, n)], engines=[mybir.EngineType.DVE], min_val=0, max_val=NODES * TILES,
                    skip_runtime_bounds_check_because="VectorE clamps the offsets where it makes them")
                return values

            def hots(slot, col0, rows_too):
                for c in range(2):
                    col = bass.ds(col0 + c, 1)
                    if rows_too:
                        V.tensor_scalar(hot_p[:, slot, c, 0:P], iota[:, 0:P], src_p[:, col], None, ALU.is_equal)
                    last = V.tensor_scalar(hot_k[:, slot, c, :], iota[:], key[:, col], None, ALU.is_equal)
                last.then_inc(hot_ready, 1)

            def add(n, b, start):
                dve.wait_ge(hist_done, n + 1)
                dve.wait_ge(hist_added, n + 3)
                win = counts[:, bass.ds(start, WCOLS)]
                V.tensor_tensor(out=win, in0=hist_ps[b][0:P, 0:WCOLS], in1=win, op=ALU.add).then_inc(hist_added, 1)

            def beside(t, q):
                if q == 1:
                    dve.wait_ge(x_landed, 16 * t + 16)
                    V.bn_stats(bn[0][:, 0, :], xin[0][:, 0:HALF])
                    step(V.bn_stats(bn[0][:, 1, :], xin[0][:, HALF:DIM]))
                    step(V.bn_aggr(mv[0][:], bn[0][:].rearrange("p a b -> p (a b)")))
                    V.tensor_scalar(mv[0][:, 1:2], mv[0][:, 1:2], LN_EPS, None, ALU.add).then_inc(var_ready, 1)
                if q == 3:
                    dve.wait_ge(std_ready, t + 1)
                    step(V.reciprocal(rstd[0][:], std[0][:]))
                    V.tensor_scalar(yn[0][:], xin[0][:], mv[0][:, 0:1], rstd[0][:], ALU.subtract, ALU.mult).then_inc(y_ready, 1)
                if q in (PER_TILE - 3, PER_TILE - 2):
                    g = q - (PER_TILE - 3)
                    dve.wait_ge(t_hi, 2 * t + g + 1)
                    V.tensor_tensor(out=xt_lo[:, t, 4 * g:4 * g + 4, :].rearrange("p k n -> p (k n)"), in0=t_ps[g][:, 0:4 * P],
                                    in1=xt_hi[:, t, 4 * g:4 * g + 4, :].rearrange("p k n -> p (k n)").bitcast(F32),
                                    op=ALU.subtract).then_inc(t_free, 1)

            step(window_starts())
            dve.wait_ge(zeroed, 1)
            starts = []
            for n in range(GROUPS + 2):
                if n < GROUPS:
                    hots(n % SLOTS, 2 * n, n % 8 == 7)
                    if n % 4 == 0:
                        starts += load_starts(n, 4)
                    beside(*divmod(n, PER_TILE))
                if n >= 2:
                    add(n - 2, (n - 2) % 3, starts[n - 2])
            rounds = dve.value_load(rnd_i[:], min_val=1, max_val=MAX_ROUNDS)
            with dve.If(rounds > 1):
                rstep = Steps(dve, round_step)
                with dve.Fori(1, rounds) as r:
                    rstep.at = (r - 1) * 3
                    rstep(V.tensor_scalar(key[:], key[:], float(-WCOLS), None, ALU.add))
                    rstep(V.tensor_scalar(base_r[:], base_r[:], float(WIN), None, ALU.add))
                    rstep(window_starts())
                    dve.sem_inc(round_begun, 1)
                    with dve.Fori(0, GROUPS) as g:
                        hots(0, 2 * g, True)
                        add(r * GROUPS + g, 0, load_starts(g, 1)[0])
            dve.wait_ge(hist_added, rounds * GROUPS + 3)
            dve.sem_inc(counts_ready, 1)
            V.tensor_reduce(indeg[:], counts[:, 0:NODES * TILES].rearrange("p (d b) -> p d b", b=TILES), AX.X, ALU.add)\
                .then_inc(indeg_ready, 1)
            dve.wait_ge(deg_done, 1)
            V.tensor_scalar(dinv[:], deg_ps[0:P, 0:TILES], 1.0, None, ALU.add).then_inc(dinv_sum, 1)
            V.tensor_reduce(dmax[:], deg_ps[0:P, 0:TILES], AX.X, ALU.max).then_inc(dmax_ready, 1)
            step(V.tensor_scalar(deg_inv[:], deg_ps[0:P, 0:TILES], 1.0, None, ALU.max))
            V.reciprocal(deg_inv[:], deg_inv[:])
            dve.wait_ge(dinv_root, 1)
            V.reciprocal(dinv[:], root[:]).then_inc(dinv_ready, 1)
            dve.wait_ge(dinv_ready, 1)
            step(V.tensor_tensor(out=dinv2[:], in0=dinv[:], in1=dinv[:], op=ALU.mult))
            dve.wait_ge(dmax_done, 1)
            step(V.tensor_scalar(big_i[:], dmax_all[0:1, :], float(EXACT), None, ALU.is_gt))
            dve.sem_inc(big_ready, 1)
            big = dve.value_load(big_i[:], min_val=0, max_val=1)
            with dve.If(big > 0):
                for n in range(2 * TILES):
                    t, part = divmod(n, 2)
                    source = counts[:, t * P * TILES:(t + 1) * P * TILES].rearrange("p (d b) -> p b d", b=TILES)
                    source = source[:, part * (TILES // 2):(part + 1) * (TILES // 2), :]
                    if n:
                        dve.wait_ge(lo_stored, 16 * n)
                    V.tensor_copy(lo_hi[:], source).then_inc(lo_step, 1)
                    dve.wait_ge(lo_step, n + 1)
                    V.tensor_tensor(out=lo_out[:], in0=source, in1=lo_hi[:].bitcast(F32), op=ALU.subtract).then_inc(lo_ready, 1)

            def stats(s, t):
                i = t % 2
                tile = acc[:, t, :] if s == 4 else x_buf(s, t)[:]
                if s == 4:
                    dve.wait_ge(acc_landed[t], 16)
                else:
                    dve.wait_ge(xin_landed[i], 16 * ((s - 1) * TILES // 2 + t // 2 + 1))
                V.bn_stats(bn[i][:, 0, :], tile[:, 0:HALF])
                step(V.bn_stats(bn[i][:, 1, :], tile[:, HALF:DIM]))
                step(V.bn_aggr(mv[i][:], bn[i][:].rearrange("p a b -> p (a b)")))
                V.tensor_scalar(mv[i][:, 1:2], mv[i][:, 1:2], LN_EPS, None, ALU.add).then_inc(var_ready, 1)

            def norm(s, t):
                i = t % 2
                tile = acc[:, t, :] if s == 4 else x_buf(s, t)[:]
                dve.wait_ge(std_ready, NORMED[s] * TILES + t + 1)
                step(V.reciprocal(rstd[i][:], std[i][:]))
                if s == 4:
                    dve.wait_ge(ps_full, job_t(s, t - 2, 1) + 1 if t >= 2 else J_STAGE[s] - 1)
                V.tensor_scalar(yn[i][:] if s == 4 else tile, tile, mv[i][:, 0:1], rstd[i][:], ALU.subtract, ALU.mult).then_inc(y_ready, 1)

            def first_rows(s):
                for t in range(2):
                    stats(s, t)
                for t in range(2):
                    norm(s, t)

            def g_low(h, t, hi, lo):
                dve.wait_ge(g_hi_done, h * TILES + t + 1)
                V.scalar_tensor_tensor(lo[:, t, :], z_raw[:, t, h * HALF:(h + 1) * HALF], dinv[:, t:t + 1],
                                       hi[:, t, 0:HALF].bitcast(F32), ALU.mult, ALU.subtract).then_inc(g_ready, 1)

            for t in range(TILES):
                dve.wait_ge(p_full, 2 * (8 if t < 5 else 9 if t < 7 else 10))
                g_low(0, t, g_hi, g_lo)
            for h in range(HALVES):
                dve.wait_ge(bias_landed, 16 * (h + 1))
                for t in range(TILES):
                    u = h * TILES + t
                    j = J_GCN + u
                    if u == HALVES * TILES - 3:
                        first_rows(1)
                    dve.wait_ge(ps_full, j + 1)
                    V.scalar_tensor_tensor(tmp[t % 2][:], bank(j)[0:P, :], dinv[:, t:t + 1],
                                           bias[:], ALU.mult, ALU.add).then_inc(ps_free, 1)
                    dve.wait_ge(ps_free, j + 1)
                    step(V.scalar_tensor_tensor(tmp[t % 2][:], z_raw[:, t, h * HALF:(h + 1) * HALF], dinv2[:, t:t + 1],
                                                tmp[t % 2][:], ALU.mult, ALU.add))
                    dve.wait_ge(res_landed[t % 2], 16 * (u // 2 + 1))
                    V.scalar_tensor_tensor(xo[t % 2][:], tmp[t % 2][:], 0.0, xo[t % 2][:], ALU.max, ALU.add).then_inc(out_ready, 1)
                    if h == 0:
                        g_low(1, t, g_hi1, g_lo1)
                dve.sem_inc(bias_used, 1)

            def lows(s, t):
                for g in range(2):
                    j = job_t(s, t, g)
                    hi = xt_hi[:, t, 4 * g:4 * g + 4, :].rearrange("p k n -> p (k n)")
                    n = 2 * t + g if s in (1, 4) or t == 0 else transposed(t, g)
                    dve.wait_ge(hi_done, HI0[s] + n + 1)
                    V.tensor_tensor(out=xt_lo[:, t, 4 * g:4 * g + 4, :].rearrange("p k n -> p (k n)"),
                                    in0=bank(j)[:, 0:4 * P], in1=hi.bitcast(F32), op=ALU.subtract).then_inc(ps_free, 1)

            def z_low(j, n, t):
                dve.wait_ge(hi_done, n + 1)
                V.tensor_tensor(out=z_lo[:, t, :], in0=bank(j)[0:P, :], in1=z_hi[:, t, :].bitcast(F32),
                                op=ALU.subtract).then_inc(ps_free, 1)

            def fused(s, first):
                for t in range(TILES + 1):
                    if s in NORMED and 2 <= t + 1 < TILES:
                        stats(s, t + 1)
                        norm(s, t + 1)
                    if t < TILES:
                        lows(s, t)
                    if t:
                        first(t - 1)

            def pre_gate(j, n, t):
                dve.wait_ge(ps_full, j + 1)
                if n >= 2:
                    dve.wait_ge(gate_done, n - 1)
                V.tensor_tensor(out=cell[:, t, :] if n % 30 < TILES else tmp[t % 2][:], in0=bank(j)[0:P, :], in1=bias[:], op=ALU.add).then_inc(ps_free, 1)
                dve.wait_ge(ps_free, j + 1)
                dve.sem_inc(pre_ready, 1)

            def first_gate(t):
                if t == 0:
                    dve.wait_ge(bias_landed, 16 * 3)
                    dve.wait_ge(counts_out, 16)
                pre_gate(J_LSTM + first_pass(t), t, t)
                if t == TILES - 1:
                    dve.sem_inc(bias_used, 1)
            fused(1, first_gate)
            for h in range(HALVES):
                for g in range(3):
                    if h == 0 and g == 0:
                        continue
                    m = 2 + 3 * h + g
                    dve.wait_ge(bias_landed, 16 * (m + 1))
                    for t in range(TILES):
                        n = 30 * h + 10 * g + t
                        if n == 56:
                            first_rows(2)
                        pre_gate(J_LSTM + FUSED + n - TILES, n, t)
                        if g == 1:
                            dve.wait_ge(gate_done, n + 1)
                            V.tensor_tensor(out=cell[:, t, :], in0=cell[:, t, :], in1=tmp[t % 2][:], op=ALU.mult).then_inc(cell_ready, 1)
                        if g == 2:
                            dve.wait_ge(gate_done, n + 1)
                            dve.wait_ge(tanh_done, 10 * h + t + 1)
                            step(V.tensor_tensor(out=tmp[t % 2][:], in0=tmp[t % 2][:], in1=cell[:, t, :], op=ALU.mult))
                            u = U0[1] + 10 * h + t
                            dve.wait_ge(res_landed[t % 2], 16 * (u // 2 + 1))
                            V.tensor_tensor(out=xo[t % 2][:], in0=tmp[t % 2][:], in1=xo[t % 2][:], op=ALU.add).then_inc(out_ready, 1)
                    dve.sem_inc(bias_used, 1)
            for layer in range(SAGE_LAYERS):
                s = 2 + layer
                j0 = J_STAGE[s]

                def z_first(t):
                    n = 3 * t + 4 if t < TILES - 1 else FUSED - 1
                    z_low(j0 + first_pass(t), HI0[s] + n, t)
                fused(s, z_first)
                for h in range(HALVES):
                    if h:
                        for t in range(TILES):
                            z_low(j0 + FUSED + 2 * TILES + t, HI0[s] + FUSED + t, t)
                    dve.wait_ge(bias_landed, 16 * (8 + 2 * layer + h + 1))
                    for t in range(TILES):
                        u = U0[s] + h * TILES + t
                        ja = j0 + FUSED + h * 3 * TILES + 2 * t
                        dve.wait_ge(ps_full, ja + 1)
                        V.scalar_tensor_tensor(tmp[t % 2][:], bank(ja)[0:P, :], deg_inv[:, t:t + 1], bias[:], ALU.mult, ALU.add).then_inc(ps_free, 1)
                        dve.wait_ge(ps_free, ja + 1)
                        if ja + 2 == J_MOE:
                            stats(4, 0)
                            norm(4, 0)
                            stats(4, 1)
                        dve.wait_ge(ps_full, ja + 2)
                        V.tensor_tensor(out=tmp[t % 2][:], in0=bank(ja + 1)[0:P, :], in1=tmp[t % 2][:], op=ALU.add).then_inc(ps_free, 1)
                        dve.wait_ge(ps_free, ja + 2)
                        if layer == 0:
                            dve.wait_ge(stored[t % 2], 16 * (u // 2))
                            V.tensor_scalar(xo[t % 2][:], tmp[t % 2][:], 0.0, None, ALU.max).then_inc(out_ready, 1)
                        else:
                            dve.wait_ge(res_landed[t % 2], 16 * ((u - TILES * 2) // 2 + 1))
                            V.tensor_tensor(out=xo[t % 2][:], in0=tmp[t % 2][:], in1=xo[t % 2][:], op=ALU.add).then_inc(out_ready, 1)
                    dve.sem_inc(bias_used, 1)
            def gate_shift(t):
                dve.wait_ge(logits_done, t + 1)
                step(V.tensor_tensor(out=lg[:, t, :], in0=ps[RING + t % 3][0:P, 0:EXPERTS], in1=gb[:], op=ALU.add))
                step(V.tensor_tensor(out=lg[:, t, :], in0=ps[RING + t % 3][0:P, EXPERTS:2 * EXPERTS], in1=lg[:, t, :], op=ALU.add))
                step(V.reduce_max(r10[:, t:t + 1], lg[:, t, :], AX.X))
                V.tensor_scalar(lg[:, t, :], lg[:, t, :], r10[:, t:t + 1], None, ALU.subtract).then_inc(shifted, 1)

            def gate_weights(t):
                r = r10[:, t:t + 1]
                dve.wait_ge(exp_done, t + 1)
                step(V.reduce_sum(r, lg[:, t, :], AX.X))
                step(V.reciprocal(r, r))
                step(V.tensor_scalar(lg[:, t, :], lg[:, t, :], r, None, ALU.mult))
                step(V.tensor_scalar(sel[:, t, :], lg[:, t, :], THRESHOLD, None, ALU.is_ge))
                step(V.tensor_tensor(out=lg[:, t, :], in0=lg[:, t, :], in1=sel[:, t, :], op=ALU.mult))
                step(V.reduce_sum(r, lg[:, t, :], AX.X))
                step(V.tensor_scalar(zero10[:, t:t + 1], r, 0.0, None, ALU.is_equal))
                step(V.tensor_tensor(out=r, in0=r, in1=zero10[:, t:t + 1], op=ALU.add))
                step(V.reciprocal(r, r))
                V.tensor_scalar(lg[:, t, :], lg[:, t, :], r, None, ALU.mult).then_inc(weights_ready, 1)
                dve.wait_ge(weights_ready, t + 1)

            def add_expert(j, b, t, h, e):
                dve.wait_ge(ps_full, j + 1)
                part = acc[:, t, h * HALF:(h + 1) * HALF]
                V.scalar_tensor_tensor(part, ps[b][0:P, :], lg[:, t, bass.ds(e, 1)], part, ALU.mult, ALU.add).then_inc(ps_free, 1)

            for t in range(TILES + 2):
                if t + 1 < TILES:
                    norm(4, t + 1)
                if t == 0:
                    dve.wait_ge(gate_in, 32)
                    step(V.tensor_copy(gw[:, :, 0, :], gw_raw[:]))
                    V.tensor_tensor(out=gw[:, :, 1, :], in0=gw_raw[:], in1=gw[:, :, 0, :].bitcast(F32), op=ALU.subtract).then_inc(gw_ready, 1)
                if t >= 2:
                    gate_weights(t - 2)
                    j = J_MOE + first_pass(t - 2)
                    add_expert(j, j % RING, t - 2, 0, 0)
                if t < TILES:
                    lows(4, t)
                if 1 <= t <= TILES:
                    gate_shift(t - 1)
                if t + 2 < TILES:
                    stats(4, t + 2)
            for t in range(TILES):
                add_expert(J_SECOND + t, t % RING, t, 1, 0)
            for h in range(HALVES):
                for t in range(TILES):
                    j = J_EXPERT_B + h * TILES + t
                    dve.wait_ge(ps_full, j + 1)
                    dve.wait_ge(ps_free, J_MOE + first_pass(t) + 1 if h == 0 else J_SECOND + t + 1)
                    part = acc[:, t, h * HALF:(h + 1) * HALF]
                    V.tensor_tensor(out=part, in0=bank(j)[0:P, :], in1=part, op=ALU.add).then_inc(ps_free, 1)
            with dve.Fori(1, EXPERTS) as e:
                for h in range(HALVES):
                    for t in range(TILES):
                        n = h * TILES + t
                        j = J_EXPERT + 2 * TILES * (e - 1) + n
                        dve.wait_ge(ps_free, j - 2 * TILES + 1)
                        add_expert(j, n % RING, t, h, e)

        @block.tensor
        def _(pe):
            mm = nc.tensor.matmul

            def hist_group(n, slot, b, added):
                pe.wait_ge(hot_ready, n + 1)
                pe.wait_ge(hist_added, added)
                for c in range(2):
                    last = mm(hist_ps[b][0:P, 0:WCOLS], hot_p[:, slot, c, 0:P], hot_k[:, slot, c, :],
                              start=c == 0, stop=c == 1)
                last.then_inc(hist_done, 1)

            PARTS = ((xt_hi, 0), (xt_hi, 1), (xt_lo, 0))

            def products(dst, t, arena, k):
                w = (w_hi[arena], w_lo[arena])
                for n, (xt, i) in enumerate(PARTS):
                    last = mm(dst[0:P, :], xt[:, t, k, :], w[i][:, k, :], start=k == 0 and n == 0, stop=k == KC - 1 and n == 2)
                return last

            def product(dst, t, arena):
                for k in range(KC):
                    last = products(dst, t, arena, k)
                return last

            def transposes(dst, y, g):
                for k in range(4):
                    c = 4 * g + k
                    last = nc.tensor.transpose(dst[:, k * P:(k + 1) * P], y[:, c * 128:(c + 1) * 128], ident[:])
                return last

            def degrees():
                rounds = pe.value_load(rnd_i[:], min_val=1, max_val=MAX_ROUNDS)
                with pe.If(rounds > 1):
                    with pe.Fori(1, rounds) as r:
                        with pe.Fori(0, GROUPS) as g:
                            hist_group(r * GROUPS + g, 0, 0, r * GROUPS + g + 3)
                pe.wait_ge(indeg_ready, 1)
                for t in range(TILES):
                    last = mm(deg_ps[0:P, t:t + 1], indeg[:, t * P:(t + 1) * P], ones[:], start=True, stop=True)
                last.then_inc(deg_done, 1)

            pe.wait_ge(const_done, 2)
            pe.wait_ge(rounds_ready, 1)
            for t in range(TILES + 2):
                for q in range(PER_TILE):
                    if t == TILES + 1 and q == KC:
                        degrees()
                    if t < TILES:
                        n = t * PER_TILE + q
                        pe.wait_ge(hot_p_ready, by_scalar(n + 1))
                        hist_group(n, n % SLOTS, n % 3, n + 1)
                    if t >= 2:
                        h, k = divmod(q, KC)
                        if q == 0:
                            pe.wait_ge(t_free, 2 * (t - 1))
                        if t == 2 and h == 1 and k == 0:
                            pe.wait_ge(part_ready, 1)
                        if t == 2 and k == h * (KC // 2):
                            pe.wait_ge(w_ready, h + 1)
                        if k == 0:
                            if t >= 4 - h:
                                pe.wait_ge(p_free, 2 * (t - 4) + 1 if h == 0 else 2 * (t - 2))
                        last = products(p_bank(t - 2, h), t - 2, h, k)
                        if k == KC - 1:
                            last.then_inc(p_full, 1)
                    if t < TILES and q == 8:
                        pe.wait_ge(y_ready, t + 1)
                        for g in range(2):
                            if t:
                                pe.wait_ge(t_free, 2 * (t - 1) + g + 1)
                            transposes(t_ps[g], yn[0], g).then_inc(t_full, 1)
            pe.wait_ge(p_full, 2 * TILES)
            nc.tensor.sem_inc(pass_done, 1)
            pe.wait_ge(big_ready, 1)
            big = pe.value_load(big_i[:], min_val=0, max_val=1)

            def free(j):
                if not (isinstance(j, int) and j < RING):
                    pe.wait_ge(ps_free, j - RING + 1)

            def aggregate(dst, t, a, hi, lo, last_rows=None):
                pe.wait_ge(a_ready, a + 1)
                for b in range(TILES):
                    if last_rows and b == TILES - 1:
                        pe.wait_ge(ps_free, last_rows)
                    if a in (0, TILES):
                        pe.wait_ge(g_ready, a + b + 1)
                    mm(dst[0:P, :], a_hi[t % 2][:, b, :], hi[:, b, :], start=b == 0, stop=False)
                    if b < TILES - 1:
                        mm(dst[0:P, :], a_hi[t % 2][:, b, :], lo[:, b, :], start=False, stop=False)
                with pe.If(big > 0):
                    for part in range(2):
                        pe.wait_ge(alo_landed, 32 * a + 16 * (part + 1))
                        for b in range(TILES // 2):
                            last = mm(dst[0:P, :], a_lo[:, b, :], hi[:, part * (TILES // 2) + b, :], start=False, stop=False)
                        last.then_inc(alo_used, 1)
                mm(dst[0:P, :], a_hi[t % 2][:, TILES - 1, :], lo[:, TILES - 1, :], start=False, stop=True).then_inc(ps_full, 1)

            for h in range(HALVES):
                for t in range(TILES):
                    j = J_GCN + h * TILES + t
                    free(j)
                    aggregate(bank(j), t, h * TILES + t, (g_hi, g_hi1)[h][:, :, 0:HALF], (g_lo, g_lo1)[h])

            def pass_end(j):
                pe.wait_ge(ps_full, j)
                nc.tensor.sem_inc(pass_done, 1)

            def gate_logits(t):
                pe.wait_ge(ps_free, job_t(4, t, 1) + 1)
                if t == 0:
                    pe.wait_ge(gw_ready, 1)
                if t >= 3:
                    pe.wait_ge(shifted, t - 2)
                for k in range(KC):
                    for n, xt in enumerate((xt_hi, xt_lo)):
                        last = mm(ps[RING + t % 3][0:P, 0:2 * EXPERTS], xt[:, t, k, :], gw[:, k].rearrange("p i e -> p (i e)"),
                                  start=k == 0 and n == 0, stop=k == KC - 1 and n == 1)
                last.then_inc(logits_done, 1)

            def fused(s, arena, n):
                for t in range(TILES + 1):
                    if t < TILES:
                        if s in NORMED:
                            pe.wait_ge(y_ready, NORMED[s] * TILES + t + 1)
                        else:
                            pe.wait_ge(xin_landed[t % 2], 16 * ((s - 1) * TILES // 2 + t // 2 + 1))
                        for g in range(2):
                            j = job_t(s, t, g)
                            free(j)
                            transposes(bank(j), yn[t % 2] if s == 4 else x_buf(s, t), g).then_inc(ps_full, 1)
                    if t == 3:
                        pe.wait_ge(ps_full, J_STAGE[s])
                        nc.tensor.sem_inc(pass_done, 1)
                    if t:
                        if s == 4:
                            gate_logits(t - 1)
                        if t == 1:
                            pe.wait_ge(w_ready, n + 1)
                        pe.wait_ge(ps_free, job_t(s, t - 1, 1) + 1)
                        j = J_STAGE[s] + first_pass(t - 1)
                        free(j)
                        product(bank(j), t - 1, arena).then_inc(ps_full, 1)
                pass_end(J_STAGE[s] + FUSED)

            fused(1, 0, N_LSTM)
            for n in range(1, 6):
                pe.wait_ge(w_ready, N_LSTM + n + 1)
                for t in range(TILES):
                    j = J_LSTM + FUSED + (n - 1) * TILES + t
                    free(j)
                    product(bank(j), t, n % 2).then_inc(ps_full, 1)
                if n < 5:
                    pass_end(j + 1)
            for layer in range(SAGE_LAYERS):
                s = 2 + layer
                n = N_SAGE[layer]
                fused(s, 0, n)
                for h in range(HALVES):
                    j0 = J_STAGE[s] + FUSED + h * 3 * TILES
                    if h:
                        pe.wait_ge(w_ready, n + 3)
                        for t in range(TILES):
                            free(j0 - TILES + t)
                            product(bank(j0 - TILES + t), t, 0).then_inc(ps_full, 1)
                        pass_end(j0)
                    pe.wait_ge(ps_free, j0 - 1)
                    pe.wait_ge(w_ready, n + 2 * h + 2)
                    for t in range(TILES):
                        ja = j0 + 2 * t
                        free(ja)
                        aggregate(bank(ja), t, A0[s] + h * TILES + t, z_hi, z_lo, None if t else j0)
                        free(ja + 1)
                        product(bank(ja + 1), t, 1).then_inc(ps_full, 1)
                    if h == 0:
                        pass_end(j0 + 2 * TILES)
            fused(4, 0, N_MOE)
            pe.wait_ge(w_ready, N_MOE + 2)
            for t in range(TILES):
                free(J_SECOND + t)
                product(bank(J_SECOND + t), t, 1).then_inc(ps_full, 1)
            pass_end(J_EXPERT_B)
            pe.wait_ge(weights_ready, TILES)
            for b in range(3):
                for t in range(4 * b, min(4 * b + 4, TILES)):
                    last = nc.tensor.transpose(ps[RING + b][0:EXPERTS, (t - 4 * b) * P:(t - 4 * b + 1) * P], lg[:, t, :], ident[:])
                last.then_inc(wt_done, 1)
            pe.wait_ge(wt_ready, 3)
            pe.wait_ge(eb_in, 16)
            for h in range(HALVES):
                for t in range(TILES):
                    j = J_EXPERT_B + h * TILES + t
                    free(j)
                    mm(bank(j)[0:P, :], wt[:, t, :], eb[:, h * HALF:(h + 1) * HALF], start=True, stop=True).then_inc(ps_full, 1)
            with pe.Fori(1, EXPERTS) as e:
                for h in range(HALVES):
                    pe.wait_ge(w_ready, N_MOE + 2 * e + h + 1)
                    for t in range(TILES):
                        n = h * TILES + t
                        j = J_EXPERT + 2 * TILES * (e - 1) + n
                        free(j)
                        product(ps[n % RING], t, h).then_inc(ps_full, 1)
                    pe.wait_ge(ps_full, j + 1)
                    nc.tensor.sem_inc(pass_done, 1)


def kernel(x, src, dst, L0_gnn_W, L0_gnn_b, L0_ffn_W_f, L0_ffn_b_f, L0_ffn_W_i, L0_ffn_b_i, L0_ffn_W_o,
           L0_ffn_b_o, L0_ffn_W_c, L0_ffn_b_c, L1_gnn_W_self0, L1_gnn_W_neigh0, L1_gnn_b0, L1_gnn_W_self1,
           L1_gnn_W_neigh1, L1_gnn_b1, L1_ffn_gate_w, L1_ffn_gate_b, L1_ffn_expert_w, L1_ffn_expert_b):
    import numpy as np
    import concourse.bacc as bacc
    from concourse.bass_utils import run_bass_kernel_spmd

    nc = bacc.Bacc("TRN2", target_bir_lowering=False, num_devices=1)
    arrays = {}

    def give(name, a):
        a = np.ascontiguousarray(a)
        arrays[name] = a
        return nc.dram_tensor(name, a.shape, mybir.dt.from_np(a.dtype), kind="ExternalInput").ap()

    src, dst = np.asarray(src), np.asarray(dst)
    args = [
        give("x_in", np.asarray(x)),
        give("src_c", src.reshape(CHUNKS, P).T),
        give("dst_c", dst.reshape(CHUNKS, P).T),
        give("dst_g", dst.reshape(2, GROUPS // 2, 2 * P).transpose(1, 0, 2)),
        give("gcn_w", np.asarray(L0_gnn_W)), give("gcn_b", np.asarray(L0_gnn_b)),
        [give(f"lstm_w{g}", np.asarray(w)[:, DIM:].T) for g, w in enumerate((L0_ffn_W_i, L0_ffn_W_c, L0_ffn_W_o))],
        [give(f"lstm_b{g}", np.asarray(b)) for g, b in enumerate((L0_ffn_b_i, L0_ffn_b_c, L0_ffn_b_o))],
        [give(f"sage_wn{i}", np.asarray(w)) for i, w in enumerate((L1_gnn_W_neigh0, L1_gnn_W_neigh1))],
        [give(f"sage_ws{i}", np.asarray(w)) for i, w in enumerate((L1_gnn_W_self0, L1_gnn_W_self1))],
        [give(f"sage_b{i}", np.asarray(b)) for i, b in enumerate((L1_gnn_b0, L1_gnn_b1))],
        give("gate_w", np.asarray(L1_ffn_gate_w)), give("gate_b", np.asarray(L1_ffn_gate_b)),
        give("expert_w", np.asarray(L1_ffn_expert_w)), give("expert_b", np.asarray(L1_ffn_expert_b)),
    ]
    out = nc.dram_tensor("out_rows", (NODES, DIM), F32, kind="ExternalOutput").ap()
    build(nc, *args, out)
    r = run_bass_kernel_spmd(nc, [arrays], core_ids=[0])
    return r.results[0]["out_rows"]
```
